# Optimizing a Trainium2 kernel written in Bass

```python
import numpy as np
import jax
import jax.numpy as jnp

def _softmax(x, axis=-1):
    return jax.nn.softmax(x, axis=axis)

def _gelu(x):
    return jax.nn.gelu(x, approximate=True)

def _silu(x):
    return jax.nn.silu(x)

def _sigmoid(x):
    return jax.nn.sigmoid(x)

def _layernorm(x, axis=-1, eps=1e-05):
    m = jnp.mean(x, axis=axis, keepdims=True)
    v = jnp.var(x, axis=axis, keepdims=True)
    return (x - m) / jnp.sqrt(v + eps)

def _scatter_add(tgt, idx, src, axis=0):
    return tgt.at[idx].add(src)

def _segment_sum(src, seg, n):
    return jax.ops.segment_sum(src, seg, n)
kernel_name = 'mk_early_fusion_d2_tok_img256_r4_63069a'

def setup_inputs(seed: int=0):
    np.random.seed(seed)
    _w = jnp.asarray

    def _rec_inputs():
        import jax
        import jax.numpy as jnp
        _rk = jax.random.key(seed)
        x = -7.10856e-05 + 0.999911 * jax.random.normal(jax.random.fold_in(_rk, 1), (8, 64, 64, 64), jnp.float32)
        txt = -0.000490742 + 0.125618 * jax.random.normal(jax.random.fold_in(_rk, 2), (8, 128, 64), jnp.float32)
        return (x, txt)
    x, txt = _rec_inputs()

    def _L0_tok_setup():
        import jax, jax.numpy as jnp
        import numpy as np
        GS = 8
        NH = 8
        DM = 64
        B, W, H = (4, 64, 64)
        key = jax.random.key(seed)
        ks = jax.random.split(key, 5)
        s = 0.02
        return {'x': jax.random.normal(ks[0], (B, DM, W, H), dtype=jnp.float32), 'Wq': jax.random.normal(ks[1], (DM, DM), dtype=jnp.float32) * s, 'bq': jnp.zeros((DM,), dtype=jnp.float32), 'Wk': jax.random.normal(ks[2], (DM, DM), dtype=jnp.float32) * s, 'bk': jnp.zeros((DM,), dtype=jnp.float32), 'Wv': jax.random.normal(ks[3], (DM, DM), dtype=jnp.float32) * s, 'bv': jnp.zeros((DM,), dtype=jnp.float32), 'Wo': jax.random.normal(ks[4], (DM, DM), dtype=jnp.float32) * s, 'bo': jnp.zeros((DM,), dtype=jnp.float32)}
    _L0_tok_all = _L0_tok_setup()
    _L0_tok_in = {k: v for k, v in _L0_tok_all.items() if k in ('Wq', 'bq', 'Wk', 'bk', 'Wv', 'bv', 'Wo', 'bo')}
    del _L0_tok_all

    def _L0_attn_setup():
        import jax, jax.numpy as jnp
        import numpy as np
        B_SZ, T, H, N, L = (4, 128, 64, 64, 4)
        EPS = 1e-05

        def _hippo(n):
            i = np.arange(n)[:, None]
            j = np.arange(n)[None, :]
            A = np.where(i >= j, (-1.0) ** (i - j) * np.sqrt((2 * i + 1.0) * (2 * j + 1.0)), 0.0)
            A = A / (1.1 * np.linalg.norm(A, 2))
            return A.astype(np.float32)

        def _xavier(key, shape):
            fan_in, fan_out = (shape[1], shape[0])
            a = float(np.sqrt(6.0 / (fan_in + fan_out)))
            return jax.random.uniform(key, shape, jnp.float32, -a, a)

        def _ln(x):
            m = jnp.mean(x, -1, keepdims=True)
            v = jnp.mean((x - m) ** 2, -1, keepdims=True)
            return (x - m) / jnp.sqrt(v + EPS)

        def _ssm_layer(h, A, B, C, D):
            Cbar = C.mean(0)
            BT = B.T
            DT = D.T

            def step(state, u):
                y = jnp.einsum('bnh,n->bh', state, Cbar) + u @ DT
                new_state = jnp.einsum('nm,bmh->bnh', A, state) + (u @ BT)[:, :, None]
                return (new_state, y)
            state0 = jnp.zeros((h.shape[0], A.shape[0], h.shape[2]), h.dtype)
            _, ys = jax.lax.scan(step, state0, jnp.swapaxes(h, 0, 1))
            y = jnp.swapaxes(ys, 0, 1)
            y = jax.nn.gelu(y, approximate=False) + h
            return _ln(y)
        key = jax.random.key(seed)
        ks = jax.random.split(key, 8)
        x = jax.random.normal(ks[0], (B_SZ, T, H), jnp.float32)
        A = jnp.broadcast_to(jnp.asarray(_hippo(N)), (L, N, N))
        Bm = jnp.stack([_xavier(jax.random.fold_in(ks[1], l), (N, H)) for l in range(L)])
        Cm = jnp.stack([_xavier(jax.random.fold_in(ks[2], l), (H, N)) for l in range(L)])
        Dm = jnp.stack([_xavier(jax.random.fold_in(ks[3], l), (H, H)) for l in range(L)])
        Win = _xavier(ks[4], (H, H))
        bin_ = jnp.zeros((H,), jnp.float32)
        Wout = _xavier(ks[5], (H, H))
        bout = jnp.zeros((H,), jnp.float32)
        return {'x': x, 'Win': Win, 'bin_': bin_, 'Wout': Wout, 'bout': bout, 'A': A, 'Bm': Bm, 'Cm': Cm, 'Dm': Dm}
    _L0_attn_all = _L0_attn_setup()
    _L0_attn_in = {k: v for k, v in _L0_attn_all.items() if k in ('Win', 'bin_', 'Wout', 'bout', 'A', 'Bm', 'Cm', 'Dm')}
    del _L0_attn_all

    def _L0_ffn_setup():
        import jax, jax.numpy as jnp
        import numpy as np
        B, S, D = (8, 1024, 64)
        H = 4 * D
        CAPACITY = 0.5
        key = jax.random.key(seed)
        ks = jax.random.split(key, 6)
        x = jax.random.normal(ks[0], (B, S, D), dtype=jnp.float32)
        attention_mask = jnp.zeros((B, 1, 1, S), dtype=jnp.float32)
        wr = jax.random.normal(ks[1], (D, 1), dtype=jnp.float32) * 0.02
        br = jnp.zeros((1,), dtype=jnp.float32)
        w1 = jax.random.normal(ks[2], (D, H), dtype=jnp.float32) * 0.02
        b1 = jnp.zeros((H,), dtype=jnp.float32)
        w2 = jax.random.normal(ks[3], (H, D), dtype=jnp.float32) * 0.02
        b2 = jnp.zeros((D,), dtype=jnp.float32)
        return {'x': x, 'attention_mask': attention_mask, 'wr': wr, 'br': br, 'w1': w1, 'b1': b1, 'w2': w2, 'b2': b2}
    _L0_ffn_all = _L0_ffn_setup()
    _L0_ffn_in = {k: v for k, v in _L0_ffn_all.items() if k in ('attention_mask', 'wr', 'br', 'w1', 'b1', 'w2', 'b2')}
    del _L0_ffn_all

    def _L1_attn_setup():
        import jax, jax.numpy as jnp
        import numpy as np
        import math
        NUM_HEADS = 8
        HEAD_SIZE = 32

        def get_alibi_slopes(n_heads):

            def pow2_slopes(n):
                start = 2.0 ** (-2.0 ** (-(math.log2(n) - 3)))
                ratio = start
                return [start * ratio ** i for i in range(n)]
            if math.log2(n_heads).is_integer():
                return np.array(pow2_slopes(n_heads), dtype=np.float32)
            cp2 = 2 ** math.floor(math.log2(n_heads))
            extra = pow2_slopes(2 * cp2)[0::2][:n_heads - cp2]
            return np.array(pow2_slopes(cp2) + extra, dtype=np.float32)
        ALIBI_SLOPES = jnp.asarray(get_alibi_slopes(NUM_HEADS))
        key = jax.random.key(seed)
        ks = jax.random.split(key, 6)
        B, T, C = (32, 128, 64)
        s = 1.0 / math.sqrt(C)
        return {'x': jax.random.normal(ks[0], (B, T, C), dtype=jnp.float32), 'Wq': jax.random.normal(ks[1], (C, NUM_HEADS * HEAD_SIZE), dtype=jnp.float32) * s, 'Wk': jax.random.normal(ks[2], (C, NUM_HEADS * HEAD_SIZE), dtype=jnp.float32) * s, 'Wv': jax.random.normal(ks[3], (C, NUM_HEADS * HEAD_SIZE), dtype=jnp.float32) * s, 'Wo': jax.random.normal(ks[4], (NUM_HEADS * HEAD_SIZE, C), dtype=jnp.float32) * s, 'bo': jax.random.normal(ks[5], (C,), dtype=jnp.float32) * 0.01}
    _L1_attn_all = _L1_attn_setup()
    _L1_attn_in = {k: v for k, v in _L1_attn_all.items() if k in ('Wq', 'Wk', 'Wv', 'Wo', 'bo')}
    del _L1_attn_all

    def _L1_ffn_setup():
        import jax, jax.numpy as jnp
        import numpy as np
        D_IN, D_HID, D_OUT = (64, 128, 64)
        N_EXPERTS, TOP_K = (64, 2)
        B, S = (8, 1024)
        key = jax.random.key(seed)
        ks = jax.random.split(key, 8)
        scale_in = 1.0 / np.sqrt(D_IN)
        scale_hid = 1.0 / np.sqrt(D_HID)
        return {'x': jax.random.normal(ks[0], (B, S, D_IN), dtype=jnp.float32), 'Wr': jax.random.uniform(ks[1], (D_IN, N_EXPERTS), jnp.float32, -scale_in, scale_in), 'br': jax.random.uniform(ks[2], (N_EXPERTS,), jnp.float32, -scale_in, scale_in), 'W1': jax.random.uniform(ks[3], (N_EXPERTS, D_IN, D_HID), jnp.float32, -scale_in, scale_in), 'b1': jax.random.uniform(ks[4], (N_EXPERTS, D_HID), jnp.float32, -scale_in, scale_in), 'W2': jax.random.uniform(ks[5], (N_EXPERTS, D_HID, D_OUT), jnp.float32, -scale_hid, scale_hid), 'b2': jax.random.uniform(ks[6], (N_EXPERTS, D_OUT), jnp.float32, -scale_hid, scale_hid)}
    _L1_ffn_all = _L1_ffn_setup()
    _L1_ffn_in = {k: v for k, v in _L1_ffn_all.items() if k in ('Wr', 'br', 'W1', 'b1', 'W2', 'b2')}
    del _L1_ffn_all
    return {'x': x, 'txt': txt, 'L0_tok_Wq': _L0_tok_in['Wq'], 'L0_tok_bq': _L0_tok_in['bq'], 'L0_tok_Wk': _L0_tok_in['Wk'], 'L0_tok_bk': _L0_tok_in['bk'], 'L0_tok_Wv': _L0_tok_in['Wv'], 'L0_tok_bv': _L0_tok_in['bv'], 'L0_tok_Wo': _L0_tok_in['Wo'], 'L0_tok_bo': _L0_tok_in['bo'], 'L0_attn_Win': _L0_attn_in['Win'], 'L0_attn_bin_': _L0_attn_in['bin_'], 'L0_attn_Wout': _L0_attn_in['Wout'], 'L0_attn_bout': _L0_attn_in['bout'], 'L0_attn_A': _L0_attn_in['A'], 'L0_attn_Bm': _L0_attn_in['Bm'], 'L0_attn_Cm': _L0_attn_in['Cm'], 'L0_attn_Dm': _L0_attn_in['Dm'], 'L0_ffn_attention_mask': _L0_ffn_in['attention_mask'], 'L0_ffn_wr': _L0_ffn_in['wr'], 'L0_ffn_br': _L0_ffn_in['br'], 'L0_ffn_w1': _L0_ffn_in['w1'], 'L0_ffn_b1': _L0_ffn_in['b1'], 'L0_ffn_w2': _L0_ffn_in['w2'], 'L0_ffn_b2': _L0_ffn_in['b2'], 'L1_attn_Wq': _L1_attn_in['Wq'], 'L1_attn_Wk': _L1_attn_in['Wk'], 'L1_attn_Wv': _L1_attn_in['Wv'], 'L1_attn_Wo': _L1_attn_in['Wo'], 'L1_attn_bo': _L1_attn_in['bo'], 'L1_ffn_Wr': _L1_ffn_in['Wr'], 'L1_ffn_br': _L1_ffn_in['br'], 'L1_ffn_W1': _L1_ffn_in['W1'], 'L1_ffn_b1': _L1_ffn_in['b1'], 'L1_ffn_W2': _L1_ffn_in['W2'], 'L1_ffn_b2': _L1_ffn_in['b2']}

def reference(x, txt, L0_tok_Wq, L0_tok_bq, L0_tok_Wk, L0_tok_bk, L0_tok_Wv, L0_tok_bv, L0_tok_Wo, L0_tok_bo, L0_attn_Win, L0_attn_bin_, L0_attn_Wout, L0_attn_bout, L0_attn_A, L0_attn_Bm, L0_attn_Cm, L0_attn_Dm, L0_ffn_attention_mask, L0_ffn_wr, L0_ffn_br, L0_ffn_w1, L0_ffn_b1, L0_ffn_w2, L0_ffn_b2, L1_attn_Wq, L1_attn_Wk, L1_attn_Wv, L1_attn_Wo, L1_attn_bo, L1_ffn_Wr, L1_ffn_br, L1_ffn_W1, L1_ffn_b1, L1_ffn_W2, L1_ffn_b2):
    import jax
    import jax.numpy as jnp

    def _L0_tok_ref(x, Wq, bq, Wk, bk, Wv, bv, Wo, bo):
        import jax, jax.numpy as jnp
        import numpy as np
        GS = 8
        NH = 8
        DM = 64
        B, W, H = (4, 64, 64)
        b, d, w, h = x.shape
        gw, gh = (w // GS, h // GS)
        n = gw * gh
        L = GS * GS
        dh = d // NH
        q = x.reshape(b, d, gw, GS, gh, GS).mean(axis=(3, 5))
        q = q.reshape(b, d, n).transpose(0, 2, 1).reshape(b * n, 1, d)
        kv = x.transpose(0, 2, 3, 1)
        kv = kv.reshape(b, gw, GS, gh, GS, d)
        kv = kv.transpose(0, 1, 3, 2, 4, 5).reshape(b * n, L, d)
        qp = (q @ Wq.T + bq).reshape(b * n, 1, NH, dh).transpose(0, 2, 1, 3)
        kp = (kv @ Wk.T + bk).reshape(b * n, L, NH, dh).transpose(0, 2, 1, 3)
        vp = (kv @ Wv.T + bv).reshape(b * n, L, NH, dh).transpose(0, 2, 1, 3)
        scores = jnp.einsum('bhqd,bhkd->bhqk', qp, kp) / jnp.sqrt(jnp.float32(dh))
        attn = jax.nn.softmax(scores, axis=-1)
        ctx = jnp.einsum('bhqk,bhkd->bhqd', attn, vp)
        ctx = ctx.transpose(0, 2, 1, 3).reshape(b * n, 1, d)
        attn_out = ctx @ Wo.T + bo
        out = q + attn_out
        return out.reshape(b, n, d)

    def _L0_attn_ref(x, Win, bin_, Wout, bout, A, Bm, Cm, Dm):
        import jax, jax.numpy as jnp
        import numpy as np
        B_SZ, T, H, N, L = (4, 128, 64, 64, 4)
        EPS = 1e-05

        def _hippo(n):
            i = np.arange(n)[:, None]
            j = np.arange(n)[None, :]
            A = np.where(i >= j, (-1.0) ** (i - j) * np.sqrt((2 * i + 1.0) * (2 * j + 1.0)), 0.0)
            A = A / (1.1 * np.linalg.norm(A, 2))
            return A.astype(np.float32)

        def _xavier(key, shape):
            fan_in, fan_out = (shape[1], shape[0])
            a = float(np.sqrt(6.0 / (fan_in + fan_out)))
            return jax.random.uniform(key, shape, jnp.float32, -a, a)

        def _ln(x):
            m = jnp.mean(x, -1, keepdims=True)
            v = jnp.mean((x - m) ** 2, -1, keepdims=True)
            return (x - m) / jnp.sqrt(v + EPS)

        def _ssm_layer(h, A, B, C, D):
            Cbar = C.mean(0)
            BT = B.T
            DT = D.T

            def step(state, u):
                y = jnp.einsum('bnh,n->bh', state, Cbar) + u @ DT
                new_state = jnp.einsum('nm,bmh->bnh', A, state) + (u @ BT)[:, :, None]
                return (new_state, y)
            state0 = jnp.zeros((h.shape[0], A.shape[0], h.shape[2]), h.dtype)
            _, ys = jax.lax.scan(step, state0, jnp.swapaxes(h, 0, 1))
            y = jnp.swapaxes(ys, 0, 1)
            y = jax.nn.gelu(y, approximate=False) + h
            return _ln(y)
        h = x @ Win.T + bin_
        for l in range(L):
            h = _ssm_layer(h, A[l], Bm[l], Cm[l], Dm[l])
        h = _ln(h)
        return h @ Wout.T + bout

    def _L0_ffn_ref(x, attention_mask, wr, br, w1, b1, w2, b2):
        import jax, jax.numpy as jnp
        import numpy as np
        B, S, D = (8, 1024, 64)
        H = 4 * D
        CAPACITY = 0.5
        b, s, d = x.shape
        weights = (jnp.einsum('bsd,do->bso', x, wr) + br)[..., 0]
        k = max(1, int(CAPACITY * s))
        kk = k - 1 if k > 1 else 1
        _, idx = jax.lax.top_k(weights, k)
        sel_idx = idx[:, :kk]
        sel = jnp.take_along_axis(x, sel_idx[:, :, None], axis=1)
        h = jax.nn.gelu(jnp.einsum('bkd,dh->bkh', sel, w1) + b1)
        y = jnp.einsum('bkh,hd->bkd', h, w2) + b2
        w_sel = jnp.take_along_axis(weights, sel_idx, axis=1)
        y = y * w_sel[..., None]
        batch_idx = jnp.arange(b)[:, None]
        processed = jnp.zeros_like(x).at[batch_idx, sel_idx].set(y)
        return processed + x

    def _L1_attn_ref(x, Wq, Wk, Wv, Wo, bo):
        import jax, jax.numpy as jnp
        import numpy as np
        import math
        NUM_HEADS = 8
        HEAD_SIZE = 32

        def get_alibi_slopes(n_heads):

            def pow2_slopes(n):
                start = 2.0 ** (-2.0 ** (-(math.log2(n) - 3)))
                ratio = start
                return [start * ratio ** i for i in range(n)]
            if math.log2(n_heads).is_integer():
                return np.array(pow2_slopes(n_heads), dtype=np.float32)
            cp2 = 2 ** math.floor(math.log2(n_heads))
            extra = pow2_slopes(2 * cp2)[0::2][:n_heads - cp2]
            return np.array(pow2_slopes(cp2) + extra, dtype=np.float32)
        ALIBI_SLOPES = jnp.asarray(get_alibi_slopes(NUM_HEADS))
        B, T, C = x.shape
        H, D = (NUM_HEADS, HEAD_SIZE)
        q = (x @ Wq).reshape(B, T, H, D).transpose(0, 2, 1, 3)
        k = (x @ Wk).reshape(B, T, H, D).transpose(0, 2, 1, 3)
        v = (x @ Wv).reshape(B, T, H, D).transpose(0, 2, 1, 3)
        scale = 1.0 / math.sqrt(D)
        wei = jnp.einsum('bhtd,bhsd->bhts', q, k) * scale
        pos = jnp.arange(T)
        rel = (pos[None, :] - pos[:, None]).astype(jnp.float32)
        bias = ALIBI_SLOPES[:, None, None] * rel[None, :, :]
        wei = wei + bias[None]
        causal = pos[None, :] <= pos[:, None]
        wei = jnp.where(causal[None, None], wei, -jnp.inf)
        wei = jax.nn.softmax(wei, axis=-1)
        out = jnp.einsum('bhts,bhsd->bhtd', wei, v)
        out = out.transpose(0, 2, 1, 3).reshape(B, T, H * D)
        return out @ Wo + bo

    def _L1_ffn_ref(x, Wr, br, W1, b1, W2, b2):
        import jax, jax.numpy as jnp
        import numpy as np
        D_IN, D_HID, D_OUT = (64, 128, 64)
        N_EXPERTS, TOP_K = (64, 2)
        B, S = (8, 1024)
        Bx, Sx, D = x.shape
        xf = x.reshape(-1, D)
        T = xf.shape[0]
        E = Wr.shape[1]
        logits = xf @ Wr + br
        topk_logits, topk_idx = jax.lax.top_k(logits, TOP_K)
        gates = jax.nn.softmax(topk_logits, axis=1)
        combine = jnp.zeros((T, E), xf.dtype).at[jnp.arange(T)[:, None], topk_idx].add(gates)
        out = jnp.zeros((T, W2.shape[-1]), xf.dtype)
        for e in range(E):
            h = jax.nn.relu(xf @ W1[e] + b1[e])
            y = h @ W2[e] + b2[e]
            out = out + combine[:, e:e + 1] * y
        return out.reshape(Bx, Sx, -1)
    h = _L0_tok_ref(x, L0_tok_Wq, L0_tok_bq, L0_tok_Wk, L0_tok_bk, L0_tok_Wv, L0_tok_bv, L0_tok_Wo, L0_tok_bo)
    h = jnp.concatenate([h, txt], axis=1)
    h = h + _L0_attn_ref(_layernorm(h, axis=-1), L0_attn_Win, L0_attn_bin_, L0_attn_Wout, L0_attn_bout, L0_attn_A, L0_attn_Bm, L0_attn_Cm, L0_attn_Dm)
    h = h + _L0_ffn_ref(_layernorm(h, axis=-1), L0_ffn_attention_mask, L0_ffn_wr, L0_ffn_br, L0_ffn_w1, L0_ffn_b1, L0_ffn_w2, L0_ffn_b2)
    h = h + _L1_attn_ref(_layernorm(h, axis=-1), L1_attn_Wq, L1_attn_Wk, L1_attn_Wv, L1_attn_Wo, L1_attn_bo)
    h = h + _L1_ffn_ref(_layernorm(h, axis=-1), L1_ffn_Wr, L1_ffn_br, L1_ffn_W1, L1_ffn_b1, L1_ffn_W2, L1_ffn_b2)
    return h

_drawn_inputs = setup_inputs


def setup_inputs(seed=0):
    import zlib

    import numpy as np

    out = dict(_drawn_inputs(seed))
    spreads = {'L0_tok_bq': (0.0, 0.8),
     'L0_tok_bk': (0.0, 0.8),
     'L0_tok_bv': (0.0, 0.1),
     'L0_tok_bo': (0.0, 0.1),
     'L0_attn_bin_': (0.0, 0.1),
     'L0_attn_bout': (0.0, 0.1),
     'L0_ffn_b1': (0.0, 0.8),
     'L0_ffn_b2': (0.0, 0.8)}
    factors = {'L0_tok_Wq': 8.0,
     'L0_tok_Wk': 8.0,
     'L0_tok_Wv': 4.332,
     'L0_attn_A': 3.414,
     'L0_ffn_wr': 8.0,
     'L0_ffn_w1': 8.0,
     'L0_ffn_w2': 8.0,
     'L1_attn_bo': 8.0,
     'L1_ffn_b1': 6.44,
     'L1_ffn_b2': 3.557}
    for name, (base, spread) in spreads.items():
        noise = np.random.default_rng([zlib.crc32(name.encode()), seed]).standard_normal(out[name].shape)
        drawn = base * np.exp(spread * noise) if base else spread * noise
        out[name] = jnp.asarray(drawn.astype(out[name].dtype))
    for name, factor in factors.items():
        out[name] = (out[name] * factor).astype(out[name].dtype)
    return out
```

```python
import numpy as np
import concourse.bass as bass
from concourse import mybir
from contextlib import ExitStack

F32 = mybir.dt.float32
BF16 = mybir.dt.bfloat16
I32 = mybir.dt.int32
U32 = mybir.dt.uint32
ALU = mybir.AluOpType
ACT = mybir.ActivationFunctionType
AX = mybir.AxisListType

B, D, IMG = 8, 64, 64
GS, NH = 8, 8
WIN = (IMG // GS) ** 2
KWIN = GS * GS
TXT = 128
T = WIN + TXT
TOK = B * T
PAIRS = B // 2
CHUNKS = WIN // 2
CK = 16
L = T // CK
NPAIR = L // 2
SSM_LAYERS = 4
EPS = 1e-5
HID = 4 * D
CAP = T // 2 - 1
AH, AD = 8, 32
HALF = T // 2
TILES = TOK // HALF
UNIT = 4 * HALF
UNITS = 6 * B
E, EH = 64, 128
EW = EH + D
BLK = 64
NBLK = (2 * TOK + E * (BLK - 1)) // BLK // 8 * 8 + 8
GB = 8
GROUPS = NBLK // GB
SLOTS = NBLK * BLK

WTOK = [("ident", 128), ("tok_WqT", 128), ("tok_Wk", 128), ("tok_WvT", 128), ("tok_WoT", 128),
        ("tok_bq", 1), ("tok_bk", 1), ("tok_bv", 1), ("tok_bo", 1), ("headsel", 16), ("headsel8", 8), ("mean", 1)]
WA = [("A", 64), ("AT", 64), ("BB", 128), ("C", 64)]
WSSM = [("WinT", 128), ("bin", 64), ("WoutT", 128), ("bout", 64)] + [(f"DT{l}", 128) for l in range(SSM_LAYERS)]
WFFN = [("wr", 64), ("br", 1), ("w1", HID), ("b1", 2), ("w2", 128), ("b2", 64), ("sameb", 128), ("isck", CK)]

WEXP = [("Wo", 2 * D), ("bo", D), ("Wr", E), ("rbr", E)]

WMOE = [("b2", D), ("before_e", E), ("upto_e", E), ("iota_m", NBLK), ("steps", TOK // BLK), ("ones", 128)]
WBIT = [("before", 128), ("ones_b", 128), ("iota_e", E)]


def offsets(cols):
    at, out = 0, {}
    for name, n in cols:
        out[name] = (at, n)
        at += n
    return out, at


def build(nc, d, out):
    with ExitStack() as ctx:
        def sb(name, shape, dt=F32):
            return ctx.enter_context(nc.sbuf_tensor(name, shape, dt))

        def sem(name):
            return ctx.enter_context(nc.semaphore(name))

        def packed(name, cols, parts=128):
            at, n = offsets(cols)
            t = sb("w_" + name, [parts, n])
            return t, (lambda key: t[:, at[key][0]:at[key][0] + at[key][1]])

        bank = [ctx.enter_context(nc.psum_tensor(f"bank{i}", [128, 512], F32)) for i in range(8)]
        img_tok = nc.dram_tensor("tokens_in", (B, T, D), F32, kind="Internal").ap()

        w_tok, wt = packed("tok", WTOK)
        w_ssm, ws = packed("ssm", WSSM)
        w_ffn, wf = packed("ffn", WFFN)
        w_a = sb("w_a", [64, SSM_LAYERS, offsets(WA)[1]])
        ident = wt("ident")

        def wa(key, l):
            at, n = offsets(WA)[0][key]
            return w_a[:, l, at:at + n]

        big = sb("big", [128, 3 * IMG * IMG])
        pixels = [big[:, IMG * IMG * u:IMG * IMG * (u + 1)] for u in range(3)]
        xw = [sb(f"windows{u}", [128, WIN, KWIN]) for u in range(2)]
        xT = [sb(f"xT{u}", [128, CHUNKS * 128]) for u in range(2)]
        q_mean = sb("q_mean", [128, PAIRS, WIN])
        heads = sb("heads", [128, 6 * 512])
        q_head = heads[:, 0:1024].rearrange("p (n j) -> p n j", j=16)
        qk_sb = heads[:, 1024:2048]
        qb_sb = sb("qb_sb", [128, 8])
        sT_sb = sb("sT_sb", [128, CHUNKS, 16])
        sc_sb = sb("sc_sb", [128, 8, 64])
        pr_sb = sb("pr_sb", [128, 8, 64])
        mx_sb = sb("mx_sb", [128, 8])
        sm_sb = sb("sm_sb", [128, 8])
        pT_sb = sb("pT_sb", [128, CHUNKS, 2, 16])
        cx_sb = heads[:, 2048:2560].rearrange("p (n h) -> p n h", h=8)
        vm_sb = heads[:, 2560:3072].rearrange("p (n h) -> p n h", h=8)
        ctx_sb = sb("ctx_sb", [128, WIN])
        hT_sb = sb("hT_sb", [128, WIN])
        hn_sb = sb("hn_sb", [64, PAIRS, 128])

        Z = sb("Z", [64, SSM_LAYERS, L, 65])
        pw = sb("pw", [64, 6, SSM_LAYERS, 2, 64])
        R = sb("R", [64, SSM_LAYERS, 4, L])
        KZ = sb("KZ", [128, SSM_LAYERS, 2 * L])
        WS = sb("WS", [128, SSM_LAYERS, NPAIR, 64])

        areas = [big[:, :]] + [t[:, :] for t in xT] + [t[:, :, :].rearrange("p n k -> p (n k)") for t in xw] + [heads[:, :]]
        taken = [0] * len(areas)

        def over(p, shape, dt=F32):
            n = int(np.prod(shape[1:])) * (2 if dt == BF16 else 4) // 4
            v = areas[p][0:shape[0], taken[p]:taken[p] + n]
            taken[p] += n
            assert taken[p] <= areas[p].shape[1]
            if dt != F32:
                v = v.bitcast(dt)
            names = "abcd"[:len(shape) - 1]
            return v.rearrange(f"p ({' '.join(names)}) -> p {' '.join(names)}", **dict(zip(names, shape[1:])))

        hL = sb("hL", [128, L, D])
        xc = over(1, [128, L, D])
        sq = over(1, [128, L, D])
        y1 = over(1, [128, L, D])
        hs = over(1, [128, L, D])
        uT = over(1, [128, NPAIR * 128])
        ln_s = sb("ln_s", [128, L])
        ln_m = sb("ln_m", [128, L])
        ln_q = sb("ln_q", [128, L])
        ln_v = sb("ln_v", [128, L])
        rstd = sb("rstd", [128, L])
        mhalf = sb("mhalf", [128, 16])
        c_sb = sb("c_sb", [128, L])
        X0 = sb("X0", [64, B, CK])
        X1 = sb("X1", [64, B, CK])
        XS = sb("XS", [64, 4, B, CK])

        x2 = over(0, [128, L, D])
        G = over(0, [128, 2, 2, NPAIR * 128])
        tok_w = over(0, [128, L])
        w_all4 = over(0, [128, CK, L])
        w_all = over(0, [128, T + L])
        ahead = over(0, [128, L, T], BF16)
        tied = over(0, [128, L, T], BF16)
        earlier = sb("earlier", [128, L, T], BF16)
        rank = over(0, [128, L])
        w_sel = over(0, [128, L])

        w_att = over(2, [64, 3, 2, 128])
        w_exp = sb("w_exp", [128, offsets(WEXP)[1]])
        x3 = over(2, [128, L, D])
        xN = over(2, [64, B, CK, L])
        alibi = over(4, [HALF, AH, T], BF16)
        identb = over(4, [HALF, HALF], BF16)
        QT = over(3, [128, 2, 2, T])
        KT = over(3, [128, 2, 2, 4, T])
        V = over(4, [HALF, 2, 2, AH, AD + 1])
        S = over(5, [HALF, 3, UNIT])
        S_max = over(1, [HALF, 3, 4])
        PT = over(4, [HALF, 2, UNIT])
        o_inv = over(1, [HALF, 2, AH])
        o_n = over(2, [HALF, 2, AH, AD])
        oT = over(5, [128, 4, HALF])
        hN = over(5, [HALF, TILES, D])

        taken[2] = taken[3] = taken[4] = 0
        W_all = big[:, :].rearrange("p (e n) -> p e n", n=EW)
        x_slots = nc.dram_tensor("x_slots", (SLOTS, D), F32, kind="Internal").ap()
        y_slots = nc.dram_tensor("y_slots", (SLOTS, D), F32, kind="Internal").ap()
        w_moe, wm = packed("moe", WMOE)
        w_bit = sb("w_bit", [128, offsets(WBIT)[1]], BF16)
        zero = sb("zero", [128, D])
        x4T = over(2, [64, L * 128])
        x4 = over(2, [128, L, D])
        logits = over(2, [128, L, E])
        top = sb("top", [128, L, 8])
        top_e = sb("top_e", [128, L, 8], U32)
        top_b = sb("top_b", [128, L, 2], BF16)
        W_sb = over(3, [128, 2, GB, EW])
        xT_sb = over(3, [EH, 2, GB * BLK])
        h_sb = over(2, [EH, 2, GB * BLK])
        x_g = over(4, [128, 2, GB // 2, D])
        y_g = over(4, [128, 2, GB // 2, D])
        OH = over(4, [128, 3, L, E], BF16)
        y_back = over(4, [128, 2, L, D])
        gate = sb("gate", [128, 4, L])
        n_blk = sb("n_blk", [64, 1])
        blk_cmp = sb("blk_cmp", [64, NBLK])
        n_bc = sb("n_bc", [64, 128])
        base = sb("base", [128, E])
        end = sb("end", [64, 1])
        slot_f = sb("slot_f", [128, 2, L])
        slot_i = sb("slot_i", [128, 3, 2, L], I32)
        addr = sb("addr", [128, 2, L], U32)
        blk_e = sb("blk_e", [1, NBLK], I32)

        def wb(key):
            at, n = offsets(WBIT)[0][key]
            return w_bit[:, at:at + n]

        def we(key):
            at, n = offsets(WEXP)[0][key]
            return w_exp[:, at:at + n]

        s = {n: sem(n) for n in """wssm_in txt_in consts_set dve_own cbar_ps pow_ps pow_ready z_ps z_ready mt_ps mt_ready r_ps r_ready
            xw_ready q_ready qp_ps qhead_ready qk_ps qk_ready qb_ready xT_ps xT_ready sT_ps sT_ready sc_ps centered
            exped probs pT_ps pT_ready cx_ps cx_ready v_ps ctx_ready o_ps hT_ready hn_ps hn_ready ln_centered
            ln_squared ln_var ln_rstd u_ready uT_ps uTa_ready uTb_ready lin_ps f_ps x_copied xs_ready c_ps y_ready
            gelu_ready hLb_ready wout_ps h_ready ff1_ps ff1_ready ff2_ps wexp_ready wall_ps wall_ready x3_ready xN_ps
            xN_ready ones_set hb_ready x4_ready x4T_ps x4T_ready logits_ps top_gap oh_ready rank_ps nblk_ready
            base_ps addr_ready blke_ps blke_ready gap_exped cmb_ready cmbT_ps cmbT_ready b2_ps b2_added zero_set
            slots_zeroed wall_in xg_seen xT8_ps xT8_ready W8_ready h8_ps h8_ready y8_ps y8_ready 
            moe_consts QKV_ps Q_ready K_ready V_ready S_ps S_centered S_exped PT_ps PT_ready PV_ps o_ready oT_ps
            oT_ready wo_ps h3_ready x2_ready hx_ready h2_ready out_done ffn_in first_in late_in res_in res_out""".split()}
        scattered = [sem(f"scattered{k}") for k in range(6)]
        gathered = [sem(f"gathered{k}") for k in range(6)]
        xg_in = [sem(f"xg_in{k}") for k in range(2)]
        y8_out = [sem(f"y8_out{k}") for k in range(2)]
        s["y_stored"], s["out_ready"] = sem("y_stored"), sem("out_ready")
        xs = [sem(f"pixels{p}_in") for p in range(PAIRS)]
        LATE = 16 * 6
        LEVELS = [(2, 1, 1), (4, 2, 2), (8, 4, 4), (12, 8, 4), (24, 12, 12), (48, 24, 24)]
        AT = {m: i for i, (m, _, _) in enumerate(LEVELS)}
        WROW = 2 * L

        def nat(m, l):
            return wa("A", l) if m == 1 else pw[:, AT[m], l, 0, :]

        def tra(m, l):
            return wa("AT", l) if m == 1 else pw[:, AT[m], l, 1, :]

        def flat(t):
            return t[:, :, :].rearrange("p i h -> p (i h)")

        def half_bank(t, k):
            return t[:, 0:8, :] if k == 0 else t[:, 8:L, :]

        def bank_tokens(k, two):
            n = 8 if k == 0 else L - 8
            return bank[two + k][:, 0:64 * n].rearrange("p (i h) -> p i h", h=D)

        def mt_bank(l):
            return 1 + 2 * (l % 3)

        def rows(k):
            return 8 if k == 0 else L - 8

        def unit_shape(n):
            return (4, HALF) if n % 3 == 0 else (2, T)

        def unit_of(n):
            slot = n % 6
            return 4 * (slot // 3) + (0, 0, 2)[slot % 3], int(slot % 3 > 0)

        def tokens_of(k):
            return xN[:, :, :, 4 * k:4 * k + 4].rearrange("p b k i -> p (b k) i")

        block = ctx.enter_context(nc.Block())

        @block.sync
        def _(sp):
            sp.dma_start(w_tok[:, :], d["w_tok"]).then_inc(s["first_in"], 16)
            sp.dma_start(w_a[:, :, :], d["w_a"]).then_inc(s["first_in"], 16)
            for p in range(PAIRS):
                if p >= 3:
                    sp.wait_ge(s["xw_ready"], 8 * (p - 2))
                sp.dma_start(pixels[p % 3][:, :], d["x"][2 * p:2 * p + 2].rearrange("b c w h -> (b c) (w h)"))\
                    .then_inc(xs[p], 16)
            sp.dma_start(img_tok[:, WIN:T, :], d["txt"]).then_inc(s["txt_in"], 16)
            sp.dma_start(w_ssm[:, :], d["w_ssm"]).then_inc(s["wssm_in"], 16)
            sp.dma_start(w_ffn[:, :], d["w_ffn"]).then_inc(s["ffn_in"], 16)
            sp.dma_start(earlier[:, :, :], d["earlier"]).then_inc(s["ffn_in"], 16)
            for p in range(PAIRS):
                sp.wait_ge(s["hn_ready"], p + 1)
                sp.dma_start(img_tok[2 * p:2 * p + 2, 0:WIN, :].rearrange("b n c -> n b c"),
                             hn_sb[:, p, :].rearrange("n (b c) -> n b c", b=2)).then_inc(s["res_out"], 16)
            sp.wait_ge(s["res_out"], 16 * PAIRS)
            sp.wait_ge(s["txt_in"], 16)
            sp.dma_start(flat(hL), img_tok.rearrange("b (k i) h -> (b k) (i h)", i=L)).then_inc(s["res_in"], 16)
            sp.wait_ge(s["hn_ready"], PAIRS)
            sp.dma_start(w_att[:, :, :, :].rearrange("p a b n -> p (a b n)"), d["w_att"]).then_inc(s["late_in"], 16)
            sp.dma_start(w_exp[:, :], d["w_exp"]).then_inc(s["late_in"], 16)
            sp.dma_start(alibi[:, :, :], d["alibi"]).then_inc(s["late_in"], 16)
            sp.dma_start(identb[:, :], d["identb"]).then_inc(s["late_in"], 16)
            sp.dma_start(w_moe[:, :], d["w_moe"]).then_inc(s["late_in"], 16)
            sp.dma_start(w_bit[:, :], d["w_bit"]).then_inc(s["late_in"], 16)
            sp.wait_ge(s["zero_set"], 1)
            sp.dma_start(x_slots.rearrange("(p q) h -> p q h", p=128),
                         zero[:, :].unsqueeze(1).broadcast_to([128, SLOTS // 128, D])).then_inc(s["slots_zeroed"], 16)
            sp.wait_ge(s["h2_ready"], 1)
            sp.dma_start(img_tok.rearrange("b (k i) h -> (b k) (i h)", i=L), flat(hL)).then_inc(s["res_out"], 16)
            sp.wait_ge(s["res_out"], 16 * (PAIRS + 1))
            sp.dma_start(hN[:, :, :], img_tok.rearrange("b (a t) h -> t (b a) h", t=HALF)).then_inc(s["res_in"], 16)
            sp.dma_start(W_all, d["w_experts"]).then_inc(s["wall_in"], 16)
            for b in range(B):
                sp.wait_ge(s["h3_ready"], b + 1)
                sp.dma_start(img_tok[b].rearrange("(a t) h -> t a h", t=HALF), hN[:, 2 * b:2 * b + 2, :]).then_inc(s["res_out"], 16)
            sp.wait_ge(s["res_out"], 16 * (PAIRS + 1 + B))
            sp.dma_start(flat(hL), img_tok.rearrange("b (k i) h -> (b k) (i h)", i=L)).then_inc(s["res_in"], 16)
            for k in range(6):
                sp.wait_ge(scattered[k], 16 * 4)
            xin = x_slots.rearrange("(p q) h -> p q h", p=128)
            yout = y_slots.rearrange("(p q) h -> p q h", p=128)
            with sp.Fori(0, GROUPS // 2) as pair:
                for u in range(2):
                    sp.wait_ge(s["xT8_ready"], pair * 2 + u + 1)
                    sp.dma_start(x_g[:, u, :, :], xin[:, bass.ds((pair * 2 + u) * (GB // 2), GB // 2), :]).then_inc(xg_in[u], 16)
            for k in range(2):
                sp.wait_ge(y8_out[k], 16 * (GROUPS // 2 + 1))
            sp.sem_inc(s["y_stored"], 1)
            for k in range(2):
                sp.wait_ge(s["out_ready"], k + 1)
                sp.dma_start(out.rearrange("b (k i) h -> (b k) i h", i=L)[:, 6 * k:6 * k + 6, :],
                             hL[:, 6 * k:6 * k + 6, :]).then_inc(s["out_done"], 16)
            sp.wait_ge(s["out_done"], 32)

        @block.gpsimd
        def _(pool):
            pool.memset(zero[:, :], 0.0).then_inc(s["zero_set"], 1)
            pool.memset(pT_sb[:, :, :, :], 0.0).then_inc(s["consts_set"], 1)
            pool.memset(KZ[:, :, :], 0.0).then_inc(s["consts_set"], 1)
            pool.memset(XS[:, :, :, :], 0.0).then_inc(s["consts_set"], 1)
            pool.memset(mhalf[:, :], -0.5).then_inc(s["consts_set"], 1)
            for p in range(PAIRS):
                pool.wait_ge(xs[p], 16)
                if p >= 2:
                    pool.wait_ge(s["sT_ps"], p - 1)
                    pool.wait_ge(s["q_ready"], p - 1)
                for gw in range(8):
                    pool.tensor_copy(xw[p % 2][:, 8 * gw:8 * gw + 8, :].rearrange("p gh (r s) -> p gh r s", r=GS),
                                     pixels[p % 3][:, 512 * gw:512 * gw + 512].rearrange("p (r gh s) -> p gh r s", r=GS, gh=8))\
                        .then_inc(s["xw_ready"], 1)
            pool.wait_ge(s["consts_set"], 4)

            def inv_std(n):
                pool.wait_ge(s["ln_var"], n + 1)
                pool.tensor_tensor(rstd[:, :], ln_v[:, :], mhalf[:, 0:L], ALU.pow).then_inc(s["ln_rstd"], 1)
            inv_std(0)
            pool.wait_ge(s["ln_centered"], 1)
            pool.wait_ge(s["wssm_in"], 16)
            pool.tensor_tensor(flat(hL).rearrange("p (i h) -> p i h", h=D), hL[:, :, :],
                               ws("bout").unsqueeze(1).broadcast_to([128, L, D]), ALU.add).then_inc(s["hLb_ready"], 1)
            for n in range(1, 6):
                inv_std(n)
            inv_std(6)
            pool.wait_ge(s["x2_ready"], 1)
            pool.tensor_tensor(hs[:, :, :], hL[:, :, :], x2[:, :, :], ALU.add).then_inc(s["hx_ready"], 1)
            inv_std(7)
            pool.memset(KT[:, :, :, :, :], 0.0).then_inc(s["ones_set"], 1)
            pool.memset(V[:, :, :, :, AD:AD + 1], 1.0).then_inc(s["ones_set"], 1)
            pool.wait_ge(s["res_in"], 32)
            pool.wait_ge(s["late_in"], LATE)
            pool.tensor_tensor(hN[:, :, :], hN[:, :, :], we("bo")[0:HALF, :].unsqueeze(1).broadcast_to([HALF, TILES, D]),
                               ALU.add).then_inc(s["hb_ready"], 1)
            inv_std(8)
            pool.wait_ge(s["h3_ready"], B)
            pool.wait_ge(s["ln_rstd"], 9)
            pool.memset(xT_sb[64:65, :, :], 1.0).then_inc(s["moe_consts"], 1)
            pool.wait_ge(s["slots_zeroed"], 16)
            pool.wait_ge(s["addr_ready"], 1)
            for k in range(2):
                for i in range(L):
                    pool.indirect_dma_start(x_slots, bass.IndirectOffsetOnAxis(addr[:, k, i:i + 1], 0), x4[:, i, :], None)\
                        .then_inc(scattered[(12 * k + i) // 4], 16)
            pool.wait_ge(s["y_stored"], 1)
            for i in range(L):
                for k in range(2):
                    pool.indirect_dma_start(y_back[:, k, i, :], None, y_slots, bass.IndirectOffsetOnAxis(addr[:, k, i:i + 1], 0))\
                        .then_inc(gathered[i // 2], 16)

        @block.scalar
        def _(act):
            copy = nc.scalar.copy

            for n in range(len(LEVELS)):
                act.wait_ge(s["pow_ps"], n + 1)
                copy(pw[:, n, :, :, :].rearrange("p l a n -> p (l a n)"), bank[0][0:64, :]).then_inc(s["pow_ready"], 1)

            def x_blocks(p):
                for g in range(CHUNKS // 4):
                    act.wait_ge(s["xT_ps"], 8 * p + g + 1)
                    if p >= 2:
                        act.wait_ge(s["cx_ps"], p - 1)
                    copy(xT[p % 2][:, 512 * g:512 * g + 512], bank[g % 2][:, :]).then_inc(s["xT_ready"], 1)
            x_blocks(0)
            for p in range(PAIRS):
                act.wait_ge(s["qk_ps"], p + 1)
                if p:
                    act.wait_ge(s["sT_ps"], p)
                copy(qk_sb[:, 0:512], bank[4][:, :])
                copy(qk_sb[:, 512:1024], bank[5][:, :]).then_inc(s["qk_ready"], 1)
                if p + 1 < PAIRS:
                    x_blocks(p + 1)
                act.wait_ge(s["centered"], p + 1)
                nc.scalar.activation(pr_sb[:, :, :], sc_sb[:, :, :], ACT.Exp, scale=float(D // NH) ** -0.5)\
                    .then_inc(s["exped"], 1)
                act.wait_ge(s["cx_ps"], p + 1)
                if p:
                    act.wait_ge(s["v_ps"], p)
                for b in range(2):
                    for k in range(2):
                        last = copy(cx_sb[64 * b:64 * b + 64, 32 * k:32 * k + 32, :],
                                    bank[2 + k][64 * b:64 * b + 64, :].rearrange("p (n b h) -> p n b h", b=2, h=8)[:, :, b, :])
                last.then_inc(s["cx_ready"], 1)
                act.wait_ge(s["hn_ps"], p + 1)
                copy(hn_sb[:, p, :], bank[6][0:64, 256:384]).then_inc(s["hn_ready"], 1)

            def squares(n, src):
                act.wait_ge(s["ln_centered"], n + 1)
                nc.scalar.activation(sq[:, :, :], src, ACT.Square).then_inc(s["ln_squared"], 1)

            def u_blocks(r):
                act.wait_ge(s["uT_ps"], r + 1)
                copy(uT[:, 0:512], bank[0][:, :]).then_inc(s["uTa_ready"], 1)
            squares(0, xc[:, :, :])
            u_blocks(0)
            u_blocks(1)
            for l in range(SSM_LAYERS):
                act.wait_ge(s["y_ready"], l + 1)
                nc.scalar.activation(sq[:, :, :], y1[:, :, :], ACT.Gelu).then_inc(s["gelu_ready"], 1)
                squares(l + 1, xc[:, :, :])
                if l + 1 < SSM_LAYERS:
                    u_blocks(l + 2)
            squares(5, xc[:, :, :])
            u_blocks(5)
            squares(6, xc[:, :, :])
            u_blocks(6)
            for g in range(4):
                par, mt = g // 2, g % 2
                for k in range(2):
                    n = 512 if k == 0 else 256
                    act.wait_ge(s["ff1_ps"], 2 * g + k + 1)
                    nc.scalar.activation(G[:, mt, par, 512 * k:512 * k + n], bank[2 + (2 * g + k) % 6][:, 0:n],
                                         ACT.Gelu_apprx_tanh, bias=wf("b1")[:, mt:mt + 1]).then_inc(s["ff1_ready"], 1)

            squares(7, xc[:, :, :])
            act.wait_ge(s["xN_ps"], 1)
            for k in range(2):
                ins = copy(tokens_of(k), bank[k][0:64, :].rearrange("p (i t) -> p t i", i=4))
            ins.then_inc(s["xN_ready"], 1)

            def query(b):
                act.wait_ge(s["QKV_ps"], 3 * b + 1)
                nc.scalar.activation(QT[:, b % 2, :, :].rearrange("p m t -> p (m t)"), bank[0][:, 0:2 * T], ACT.Copy,
                                     scale=float(AD) ** -0.5).then_inc(s["Q_ready"], 1)

            def key(b):
                act.wait_ge(s["QKV_ps"], 3 * b + 2)
                for k in (2, 3):
                    q = slice(AD * k, AD * k + AD)
                    ins = copy(KT[q, b % 2, :, k, :], bank[0][q, 0:2 * T].rearrange("p (m t) -> p m t", m=2))
                ins.then_inc(s["K_ready"], 1)
            query(0)
            act.wait_ge(s["ones_set"], 2)
            key(0)
            for n in range(UNITS + 4):
                b, slot = divmod(n, 6)
                if n < UNITS:
                    act.wait_ge(s["S_centered"], n + 1)
                    nc.scalar.activation(S[:, n % 3, :], S[:, n % 3, :], ACT.Exp).then_inc(s["S_exped"], 1)
                if b + 1 < B and slot == 0:
                    query(b + 1)
                if b + 1 < B and slot == 1:
                    key(b + 1)
                if b and slot == 3:
                    act.wait_ge(s["oT_ps"], b)
                    copy(oT[:, :, :].rearrange("p a t -> p (a t)"), bank[0][:, 0:4 * HALF]).then_inc(s["oT_ready"], 1)
                if 1 <= n <= UNITS:
                    act.wait_ge(s["PT_ps"], n)
                    if n >= 3:
                        act.wait_ge(s["PV_ps"], n - 2)
                    copy(PT[:, (n - 1) % 2, :], bank[3 + (n - 1) % 2][0:HALF, 0:UNIT]).then_inc(s["PT_ready"], 1)

            squares(8, xc[:, :, :])
            act.wait_ge(s["x4T_ps"], 1)
            for k in range(2):
                ins = copy(x4T[:, 512 * k:512 * k + 512], bank[k][0:64, :])
            ins.then_inc(s["x4T_ready"], 1)
            act.wait_ge(s["top_gap"], 1)
            nc.scalar.activation(gate[:, 1, :], gate[:, 0, :], ACT.Exp).then_inc(s["gap_exped"], 1)
            act.wait_ge(s["cmbT_ps"], 1)
            for k in range(2):
                ins = copy(x4T[:, 512 * k:512 * k + 512], bank[k][0:64, :])
            ins.then_inc(s["cmbT_ready"], 1)
            act.wait_ge(s["moe_consts"], 1)
            act.wait_ge(s["b2_ps"], 1)
            act.sem_inc(s["xT8_ready"], 2)
            with act.Fori(0, GROUPS // 2) as pair:
                for u in range(2):
                    g = pair * 2 + u
                    act.wait_ge(s["xT8_ps"], g + 1)
                    copy(xT_sb[0:64, u, :], bank[u][0:64, :]).then_inc(s["xT8_ready"], 1)
                    act.wait_ge(s["h8_ps"], g + 1)
                    nc.scalar.activation(h_sb[:, u, :], bank[2 + u][:, :], ACT.Relu).then_inc(s["h8_ready"], 1)
                    act.wait_ge(s["y8_ready"], g + 3)
                    act.dma_start(y_slots.rearrange("(p q) h -> p q h", p=128)[:, bass.ds(g * (GB // 2), GB // 2), :],
                                  y_g[:, u, :, :]).then_inc(y8_out[u], 16)

        @block.vector
        def _(dve):
            done = [0]

            def link(ins):
                done[0] += 1
                ins.then_inc(s["dve_own"], 1)
                dve.wait_ge(s["dve_own"], done[0])
            tt, ts = nc.vector.tensor_tensor, nc.vector.tensor_scalar
            copy, red = nc.vector.tensor_copy, nc.vector.tensor_reduce

            dve.wait_ge(s["first_in"], 32)
            for l in range(SSM_LAYERS):
                copy(Z[:, l, 0, 0:64], ident[0:64, 0:64])
            dve.wait_ge(s["cbar_ps"], 1)
            copy(Z[:, :, 0, 64], bank[7][0:64, 0:SSM_LAYERS]).then_inc(s["z_ready"], 1)
            for n, m in enumerate((1, 2, 4, 8)):
                k = min(m, L - m)
                dve.wait_ge(s["z_ps"], n + 1)
                for l in range(SSM_LAYERS):
                    ins = copy(Z[:, l, m:m + k, :], bank[1 + l][0:64, 0:65 * k].rearrange("p (j n) -> p j n", n=65))
                ins.then_inc(s["z_ready"], 1)
            dve.wait_ge(s["z_ready"], 5)
            copy(R[:, :, 0, :], Z[:, :, :, 64]).then_inc(s["r_ready"], 1)

            def mt_copies(l):
                dve.wait_ge(s["mt_ps"], l + 1)
                k = mt_bank(l)
                for half in range(2):
                    q = slice(64 * half, 64 * half + 64)
                    odd = 1 - half
                    copy(WS[q, l, 0:4, :], bank[k][q, :].rearrange("p (j a n) -> p j a n", a=2, n=64)[:, :, odd, :])
                    copy(WS[q, l, 4:6, :], bank[k + 1][q, 0:256].rearrange("p (j a n) -> p j a n", a=2, n=64)[:, :, odd, :])
                    ins = copy(KZ[q, l, L + half:2 * L - 1 + half], bank[k + 1][q, 256:256 + L - 1])
                ins.then_inc(s["mt_ready"], 1)
            dve.wait_ge(s["consts_set"], 4)
            for l in range(SSM_LAYERS):
                mt_copies(l)
            for k in range(1, 4):
                dve.wait_ge(s["r_ps"], k)
                copy(R[:, :, k, :], bank[7][0:64, 0:SSM_LAYERS * L].rearrange("p (l j) -> p l j", j=L)).then_inc(s["r_ready"], 1)

            def means(p):
                for gw in range(8):
                    dve.wait_ge(s["xw_ready"], 8 * p + gw + 1)
                    ins = red(q_mean[:, p, :].rearrange("p (g w c) -> p g c w", g=4, w=2)[:, gw // 2, 4 * (gw % 2):4 * (gw % 2) + 4, :],
                              xw[p % 2][:, 8 * gw:8 * gw + 8, :].rearrange("p (c w) k -> p c w k", w=2), AX.X, ALU.add)
                link(ins)
                ts(q_mean[:, p, :], q_mean[:, p, :], 1.0 / KWIN, None, ALU.mult).then_inc(s["q_ready"], 1)
            means(0)
            for p in range(PAIRS):
                dve.wait_ge(s["qp_ps"], p + 1)
                nc.vector.scalar_tensor_tensor(
                    q_head[:, :, :], bank[6][:, 0:WIN].unsqueeze(2).broadcast_to([128, WIN, 16]), wt("tok_bq"),
                    wt("headsel").unsqueeze(1).broadcast_to([128, WIN, 16]), ALU.add, ALU.mult).then_inc(s["qhead_ready"], 1)
                dve.wait_ge(s["qk_ps"], p + 1)
                copy(qb_sb[:, :], bank[6][:, 64:72]).then_inc(s["qb_ready"], 1)
                dve.wait_ge(s["sT_ps"], p + 1)
                for w in range(2):
                    for k in range(2):
                        ins = copy(sT_sb[64 * w:64 * w + 64, 16 * k:16 * k + 16, :],
                                   bank[2 + k][64 * w:64 * w + 64, :].rearrange("p (c w j) -> p c w j", w=2, j=16)[:, :, w, :])
                ins.then_inc(s["sT_ready"], 1)
                dve.wait_ge(s["sc_ps"], p + 1)
                dve.wait_ge(s["qb_ready"], p + 1)
                link(tt(sc_sb[:, :, :], bank[5][:, :].rearrange("p (g k) -> p g k", k=64),
                        qb_sb[:, :].unsqueeze(2).broadcast_to([128, 8, 64]), ALU.add))
                link(red(mx_sb[:, :], sc_sb[:, :, :], AX.X, ALU.max))
                tt(sc_sb[:, :, :], sc_sb[:, :, :], mx_sb[:, :].unsqueeze(2).broadcast_to([128, 8, 64]), ALU.subtract)\
                    .then_inc(s["centered"], 1)
                dve.wait_ge(s["exped"], p + 1)
                link(red(sm_sb[:, :], pr_sb[:, :, :], AX.X, ALU.add))
                link(nc.vector.reciprocal(sm_sb[:, :], sm_sb[:, :]))
                tt(pr_sb[:, :, :], pr_sb[:, :, :], sm_sb[:, :].unsqueeze(2).broadcast_to([128, 8, 64]), ALU.mult)\
                    .then_inc(s["probs"], 1)
                dve.wait_ge(s["pT_ps"], p + 1)
                if p:
                    dve.wait_ge(s["cx_ps"], p)
                for w in range(2):
                    ins = copy(pT_sb[64 * w:64 * w + 64, :, w, :],
                               bank[7][64 * w:64 * w + 64, :].rearrange("p (c j) -> p c j", j=16))
                ins.then_inc(s["pT_ready"], 1)
                if p + 1 < PAIRS:
                    means(p + 1)
                dve.wait_ge(s["v_ps"], p + 1)
                link(tt(vm_sb[:, :, :], bank[4][:, :].rearrange("p (n h) -> p n h", h=8),
                        wt("headsel8").unsqueeze(1).broadcast_to([128, WIN, 8]), ALU.mult))
                link(red(ctx_sb[:, :], vm_sb[:, :, :], AX.X, ALU.add))
                ts(ctx_sb[:, :], ctx_sb[:, :], wt("tok_bv"), None, ALU.add).then_inc(s["ctx_ready"], 1)
                dve.wait_ge(s["o_ps"], p + 1)
                link(ts(ctx_sb[:, :], bank[6][:, 128:192], wt("tok_bo"), None, ALU.add))
                order = "p (g c w) -> p g c w"
                tt(hT_sb[:, :].rearrange(order, g=4, w=2), ctx_sb[:, :].rearrange(order, g=4, w=2),
                   q_mean[:, p, :].rearrange("p (g w c) -> p g c w", g=4, w=2), ALU.add).then_inc(s["hT_ready"], 1)

            def norm(n, src, dst, then):
                link(red(ln_s[:, :], src, AX.X, ALU.add))
                link(ts(ln_m[:, :], ln_s[:, :], 1.0 / D, None, ALU.mult))
                tt(xc[:, :, :], src, ln_m[:, :].unsqueeze(2).broadcast_to([128, L, D]), ALU.subtract)\
                    .then_inc(s["ln_centered"], 1)
                dve.wait_ge(s["ln_squared"], n + 1)
                link(red(ln_q[:, :], sq[:, :, :], AX.X, ALU.add))
                ts(ln_v[:, :], ln_q[:, :], 1.0 / D, EPS, ALU.mult, ALU.add).then_inc(s["ln_var"], 1)
                dve.wait_ge(s["ln_rstd"], n + 1)
                dve.wait_ge(s["ln_centered"], n + 1)
                tt(dst, xc[:, :, :], rstd[:, :].unsqueeze(2).broadcast_to([128, L, D]), ALU.mult).then_inc(s[then], 1)

            def u_blocks(r):
                dve.wait_ge(s["uT_ps"], r + 1)
                copy(uT[:, 512:768], bank[1][:, 0:256]).then_inc(s["uTb_ready"], 1)
            dve.wait_ge(s["res_in"], 16)
            norm(0, hL[:, :, :], y1[:, :, :], "u_ready")
            u_blocks(0)
            dve.wait_ge(s["lin_ps"], 1)
            for k in range(2):
                ins = tt(half_bank(hs, k), bank_tokens(k, 2), ws("bin").unsqueeze(1).broadcast_to([128, rows(k), D]), ALU.add)
            ins.then_inc(s["u_ready"], 1)
            u_blocks(1)
            for l in range(SSM_LAYERS):
                state = bank[5][0:64, 0:128].rearrange("p (b k) -> p b k", k=CK)
                for k, dst in enumerate((X0, X1)):
                    dve.wait_ge(s["f_ps"], 3 * l + k + 1)
                    copy(dst[:, :, :], state).then_inc(s["x_copied"], 1)
                dve.wait_ge(s["f_ps"], 3 * l + 3)
                for k in range(4):
                    by = 1 + 4 * k
                    ins = copy(XS[:, k, :, by:CK], state[:, :, 0:CK - by])
                ins.then_inc(s["xs_ready"], 1)
                dve.wait_ge(s["c_ps"], l + 1)
                link(copy(c_sb[:, :], bank[4][:, 0:L]))
                for k in range(2):
                    ins = tt(half_bank(y1, k), bank_tokens(k, 2),
                             (c_sb[:, 0:8] if k == 0 else c_sb[:, 8:L]).unsqueeze(2).broadcast_to([128, rows(k), D]), ALU.add)
                ins.then_inc(s["y_ready"], 1)
                dve.wait_ge(s["gelu_ready"], l + 1)
                link(tt(y1[:, :, :], sq[:, :, :], hs[:, :, :], ALU.add))
                norm(l + 1, y1[:, :, :], hs[:, :, :], "u_ready")
                if l + 1 < SSM_LAYERS:
                    u_blocks(l + 2)
            dve.wait_ge(s["u_ready"], 2 + SSM_LAYERS)
            norm(5, hs[:, :, :], y1[:, :, :], "u_ready")
            u_blocks(5)
            dve.wait_ge(s["wout_ps"], 1)
            dve.wait_ge(s["hLb_ready"], 1)
            for k in range(2):
                ins = tt(half_bank(hL, k), bank_tokens(k, 2), half_bank(hL, k), ALU.add)
            ins.then_inc(s["h_ready"], 1)

            dve.wait_ge(s["h_ready"], 1)
            norm(6, hL[:, :, :], x2[:, :, :], "x2_ready")
            u_blocks(6)
            dve.wait_ge(s["x2_ready"], 1)
            dve.wait_ge(s["ffn_in"], 32)
            link(tt(xc[:, :, :], x2[:, :, :], wf("wr").unsqueeze(1).broadcast_to([128, L, D]), ALU.mult))
            link(red(tok_w[:, :], xc[:, :, :], AX.X, ALU.add))
            link(ts(tok_w[:, :], tok_w[:, :], wf("br"), None, ALU.add))
            tt(w_all4[:, :, :], tok_w[:, :].unsqueeze(1).broadcast_to([128, CK, L]),
               wf("isck").unsqueeze(2).broadcast_to([128, CK, L]), ALU.mult).then_inc(s["wexp_ready"], 1)
            dve.wait_ge(s["wall_ps"], 1)
            copy(w_all[:, :], bank[1][:, 256:256 + T + L]).then_inc(s["wall_ready"], 1)
            dve.wait_ge(s["wall_ready"], 1)
            every = w_all[:, 0:T].unsqueeze(1).broadcast_to([128, L, T])
            own = w_all[:, T:T + L].unsqueeze(2).broadcast_to([128, L, T])
            tt(ahead[:, :, :], every, own, ALU.is_gt)
            link(tt(tied[:, :, :], every, own, ALU.is_ge))
            dve.wait_ge(s["ffn_in"], 32)
            link(tt(tied[:, :, :], tied[:, :, :], earlier[:, :, :], ALU.mult))
            link(tt(ahead[:, :, :], ahead[:, :, :], tied[:, :, :], ALU.max))
            link(red(rank[:, :], ahead[:, :, :], AX.X, ALU.add))
            link(nc.vector.scalar_tensor_tensor(w_sel[:, :], rank[:, :], float(CAP), tok_w[:, :], ALU.is_lt, ALU.mult))
            dve.wait_ge(s["ff2_ps"], 1)
            for k in range(2):
                ins = tt(half_bank(y1, k), bank_tokens(k, 0), wf("b2").unsqueeze(1).broadcast_to([128, rows(k), D]), ALU.add)
            link(ins)
            link(tt(y1[:, :, :], y1[:, :, :], w_sel[:, :].unsqueeze(2).broadcast_to([128, L, D]), ALU.mult))
            dve.wait_ge(s["hx_ready"], 1)
            tt(hL[:, :, :], y1[:, :, :], hs[:, :, :], ALU.add).then_inc(s["h2_ready"], 1)

            dve.wait_ge(s["h2_ready"], 1)
            norm(7, hL[:, :, :], x3[:, :, :], "x3_ready")
            dve.wait_ge(s["xN_ps"], 1)
            copy(tokens_of(2), bank[2][0:64, :].rearrange("p (i t) -> p t i", i=4)).then_inc(s["xN_ready"], 1)

            def value(b):
                dve.wait_ge(s["QKV_ps"], 3 * b + 3)
                copy(V[:, b % 2, :, :, 0:AD], bank[0][0:HALF, :].rearrange("p (a h d) -> p a h d", a=2, h=AH))\
                    .then_inc(s["V_ready"], 1)

            def key(b):
                dve.wait_ge(s["QKV_ps"], 3 * b + 2)
                for k in (0, 1):
                    q = slice(AD * k, AD * k + AD)
                    ins = copy(KT[q, b % 2, :, k, :], bank[0][q, 0:2 * T].rearrange("p (m t) -> p m t", m=2))
                ins.then_inc(s["K_ready"], 1)
            dve.wait_ge(s["ones_set"], 2)
            key(0)
            value(0)
            for n in range(UNITS + 5):
                b, slot = divmod(n, 6)
                if b and slot == 2:
                    dve.wait_ge(s["PV_ps"], 6 * b)
                    if b >= 2:
                        dve.wait_ge(s["oT_ps"], b - 1)
                    for a in range(2):
                        o = bank[1 + a][0:HALF, 0:AH * (AD + 1)].rearrange("p (h d) -> p h d", h=AH)
                        link(nc.vector.reciprocal(o_inv[:, a, :], o[:, :, AD]))
                        ins = tt(o_n[:, a, :, :], o[:, :, 0:AD], o_inv[:, a, :].unsqueeze(2).broadcast_to([HALF, AH, AD]), ALU.mult)
                    ins.then_inc(s["o_ready"], 1)
                if n < UNITS:
                    heads, keys = unit_shape(n)
                    dve.wait_ge(s["S_ps"], n + 1)
                    scores = bank[5 + n % 3][0:HALF, 0:UNIT].rearrange("p (h k) -> p h k", h=heads)
                    link(red(S_max[:, n % 3, 0:heads], scores, AX.X, ALU.max))
                    if n >= 3:
                        dve.wait_ge(s["PT_ps"], n - 2)
                    tt(S[:, n % 3, :].rearrange("p (h k) -> p h k", h=heads), scores,
                       S_max[:, n % 3, 0:heads].unsqueeze(2).broadcast_to([HALF, heads, keys]), ALU.subtract)\
                        .then_inc(s["S_centered"], 1)
                if b + 1 < B and slot == 1:
                    key(b + 1)
                if b + 1 < B and slot == 2:
                    value(b + 1)
                if b and slot == 4:
                    dve.wait_ge(s["wo_ps"], b)
                    dve.wait_ge(s["hb_ready"], 1)
                    h = hN[:, 2 * b - 2:2 * b, :]
                    tt(h, bank[0][0:HALF, 0:2 * D].rearrange("p (a h) -> p a h", a=2), h, ALU.add).then_inc(s["h3_ready"], 1)

            dve.wait_ge(s["res_in"], 48)
            norm(8, hL[:, :, :], x4[:, :, :], "x4_ready")
            dve.wait_ge(s["x4T_ps"], 1)
            copy(x4T[:, 1024:1536], bank[2][0:64, :]).then_inc(s["x4T_ready"], 1)
            dve.wait_ge(s["late_in"], LATE)
            dve.wait_ge(s["logits_ps"], 1)
            for k in range(2):
                ins = tt(half_bank(logits, k), bank_tokens(k, 3), we("rbr").unsqueeze(1).broadcast_to([128, rows(k), D]), ALU.add)
            link(ins)
            for i in range(L):
                ins = nc.vector.max(top[:, i, :], logits[:, i, :])
            link(ins)
            for i in range(L):
                ins = nc.vector.max_index(top_e[:, i, :], top[:, i, :], logits[:, i, :])
            link(ins)
            tt(gate[:, 0, :], top[:, :, 1], top[:, :, 0], ALU.subtract).then_inc(s["top_gap"], 1)
            link(copy(top_b[:, :, :], top_e[:, :, 0:2]))
            for k in range(2):
                ins = tt(OH[:, k, :, :], wb("iota_e").unsqueeze(1).broadcast_to([128, L, E]),
                         top_b[:, :, k].unsqueeze(2).broadcast_to([128, L, E]), ALU.is_equal)
            link(ins)
            tt(OH[:, 2, :, :], OH[:, 0, :, :], OH[:, 1, :, :], ALU.add).then_inc(s["oh_ready"], 1)
            dve.wait_ge(s["gap_exped"], 1)
            link(ts(gate[:, 0, :], gate[:, 1, :], 1.0, None, ALU.add))
            link(nc.vector.reciprocal(gate[:, 2, :], gate[:, 0, :]))
            tt(gate[:, 3, :], gate[:, 2, :], gate[:, 1, :], ALU.mult)
            dve.wait_ge(s["rank_ps"], 1)
            link(tt(blk_cmp[:, 0:TOK // BLK], bank[7][0:64, 0:1].broadcast_to([64, TOK // BLK]), wm("steps")[0:64, :], ALU.is_gt))
            link(red(n_blk[:, :], blk_cmp[:, 0:TOK // BLK], AX.X, ALU.add))
            ts(n_bc[:, :], wm("ones")[0:64, :], n_blk[:, 0:1], None, ALU.mult).then_inc(s["nblk_ready"], 1)
            dve.wait_ge(s["base_ps"], 1)
            link(copy(base[:, :], bank[7][:, 64:128]))
            link(copy(end[:, :], bank[7][0:64, 1:2]))
            ts(blk_cmp[:, :], wm("iota_m")[0:64, :], end[:, 0:1], None, ALU.is_ge).then_inc(s["nblk_ready"], 1)
            for k in range(2):
                ins = tt(half_bank(xc, k), bank_tokens(k, 5), base[:, :].unsqueeze(1).broadcast_to([128, rows(k), D]), ALU.add)
            link(ins)
            for k in range(2):
                link(tt(sq[:, :, :], xc[:, :, :], OH[:, k, :, :], ALU.mult))
                link(red(slot_f[:, k, :], sq[:, :, :], AX.X, ALU.add))
            link(copy(slot_i[:, 0, :, :], slot_f[:, :, :]))
            ts(slot_i[:, 1, :, :], slot_i[:, 0, :, :], 127, None, ALU.bitwise_and)
            link(ts(slot_i[:, 2, :, :], slot_i[:, 0, :, :], 7, None, ALU.logical_shift_right))
            nc.vector.scalar_tensor_tensor(addr[:, :, :], slot_i[:, 1, :, :], float(SLOTS // 128), slot_i[:, 2, :, :],
                                           ALU.mult, ALU.add).then_inc(s["addr_ready"], 1)
            dve.wait_ge(s["blke_ps"], 1)
            ts(blk_e[:, :], bank[7][0:1, 128:128 + NBLK], float(E - 1), None, ALU.min).then_inc(s["blke_ready"], 1)
            dve.wait_ge(s["addr_ready"], 1)
            link(tt(xc[:, :, :], OH[:, 0, :, :], gate[:, 2, :].unsqueeze(2).broadcast_to([128, L, E]), ALU.mult))
            link(tt(sq[:, :, :], OH[:, 1, :, :], gate[:, 3, :].unsqueeze(2).broadcast_to([128, L, E]), ALU.mult))
            tt(y1[:, :, :], xc[:, :, :], sq[:, :, :], ALU.add).then_inc(s["cmb_ready"], 1)
            dve.wait_ge(s["cmbT_ps"], 1)
            copy(x4T[:, 1024:1536], bank[2][0:64, :]).then_inc(s["cmbT_ready"], 1)
            dve.wait_ge(s["b2_ps"], 1)
            for k in range(2):
                ins = tt(half_bank(hL, k), bank_tokens(k, 3), half_bank(hL, k), ALU.add)
            ins.then_inc(s["b2_added"], 1)
            dve.wait_ge(s["wall_in"], 16)
            dve.wait_ge(s["blke_ready"], 1)
            dve.sem_inc(s["y8_ready"], 2)
            for k in range(2):
                dve.sem_inc(y8_out[k], 16)
            regs = [dve.alloc_register(f"expert{k}") for k in range(GB)]
            with dve.Fori(0, GROUPS // 2) as pair:
                for u in range(2):
                    g = pair * 2 + u
                    dve.load(regs, blk_e[0:1, bass.ds(g * GB, GB)])
                    for k in range(GB):
                        e = dve.snap(regs[k], min_val=0, max_val=E - 1)
                        ins = copy(W_sb[:, u, k, :], big[:, bass.ds(e * EW, EW)])
                    ins.then_inc(s["W8_ready"], 1)
                    dve.wait_ge(s["y8_ps"], g + 1)
                    dve.wait_ge(y8_out[u], pair * 16 + 16)
                    copy(y_g[:, u, :, :], bank[4 + u][:, 0:256].rearrange("p (q h) -> p q h", h=D)).then_inc(s["y8_ready"], 1)
            dve.wait_ge(s["b2_added"], 1)
            for i in range(L):
                if i % 2 == 0:
                    dve.wait_ge(gathered[i // 2], 16 * 4)
                link(nc.vector.scalar_tensor_tensor(hL[:, i, :], y_back[:, 0, i, :], gate[:, 2, i:i + 1], hL[:, i, :], ALU.mult, ALU.add))
                ins = nc.vector.scalar_tensor_tensor(hL[:, i, :], y_back[:, 1, i, :], gate[:, 3, i:i + 1], hL[:, i, :], ALU.mult, ALU.add)
                if i % 6 == 5:
                    ins.then_inc(s["out_ready"], 1)

        @block.tensor
        def _(pe):
            def mm(out, lhsT, rhs, start=True, stop=True, **kw):
                return nc.tensor.matmul(out, lhsT, rhs, start=start, stop=stop, **kw)

            def transpose(out, in_, n):
                return nc.tensor.transpose(out, in_, ident[0:n, 0:n])

            pe.wait_ge(s["first_in"], 32)
            for l in range(SSM_LAYERS):
                ins = mm(bank[7][0:64, l:l + 1], wa("C", l), wt("mean")[0:64, :])
            ins.then_inc(s["cbar_ps"], 1)

            def level(n):
                m, a, b = LEVELS[n]
                if n:
                    pe.wait_ge(s["pow_ready"], n)
                for l in range(SSM_LAYERS):
                    mm(bank[0][0:64, 128 * l:128 * l + 64], tra(a, l), nat(b, l))
                    ins = mm(bank[0][0:64, 128 * l + 64:128 * l + 128], nat(b, l), tra(a, l))
                ins.then_inc(s["pow_ps"], 1)

            def extend(n):
                m = 1 << n
                k = min(m, L - m)
                pe.wait_ge(s["z_ready"], n + 1)
                for l in range(SSM_LAYERS):
                    ins = mm(bank[1 + l][0:64, 0:65 * k], nat(m, l), Z[:, l, 0:k, :])
                ins.then_inc(s["z_ps"], 1)
            for n in range(4):
                level(n)
                extend(n)
            level(4)
            pe.wait_ge(s["z_ready"], 5)
            for l in range(SSM_LAYERS):
                if l == 3:
                    pe.wait_ge(s["mt_ready"], 1)
                k = mt_bank(l)
                mm(bank[k][:, :], wa("BB", l), Z[:, l, 0:8, 0:64])
                mm(bank[k + 1][:, 0:256], wa("BB", l), Z[:, l, 8:12, 0:64])
                mm(bank[k + 1][:, 256:256 + L - 1], wa("BB", l), Z[:, l, 0:L - 1, 64]).then_inc(s["mt_ps"], 1)
            level(5)
            pe.wait_ge(s["pow_ready"], 6)
            for k in range(1, 4):
                pe.wait_ge(s["r_ready"], k)
                for l in range(SSM_LAYERS):
                    ins = mm(bank[7][0:64, L * l:L * l + L], nat(48, l), R[:, l, k - 1, :])
                ins.then_inc(s["r_ps"], 1)

            def chunk(p, c):
                return xw[p % 2][:, 2 * c:2 * c + 2, :].rearrange("p n k -> p (n k)")

            def x_blocks(p):
                for g in range(CHUNKS // 4):
                    pe.wait_ge(s["xw_ready"], 8 * p + g + 1)
                    n = 8 * p + g
                    if n >= 2:
                        pe.wait_ge(s["xT_ready"], n - 1)
                    for k in range(4):
                        ins = transpose(bank[g % 2][:, 128 * k:128 * k + 128], chunk(p, 4 * g + k), 128)
                    ins.then_inc(s["xT_ps"], 1)
            x_blocks(0)
            for p in range(PAIRS):
                pe.wait_ge(s["q_ready"], p + 1)
                if p:
                    pe.wait_ge(s["hn_ready"], p)
                    pe.wait_ge(s["hT_ready"], p)
                mm(bank[6][:, 0:WIN], wt("tok_WqT"), q_mean[:, p, :]).then_inc(s["qp_ps"], 1)
                pe.wait_ge(s["qhead_ready"], p + 1)
                if p:
                    pe.wait_ge(s["centered"], p)
                    pe.wait_ge(s["ctx_ready"], p)
                qh = q_head[:, :, :].rearrange("p n j -> p (n j)")
                mm(bank[4][:, :], wt("tok_Wk"), qh[:, 0:512])
                mm(bank[5][:, :], wt("tok_Wk"), qh[:, 512:1024])
                for g in range(4):
                    for w in range(2):
                        ins = mm(bank[6][:, 64 + 2 * g + w:65 + 2 * g + w], qh[:, 128 * (2 * g + w):128 * (2 * g + w) + 128],
                                 wt("tok_bk"))
                ins.then_inc(s["qk_ps"], 1)
                pe.wait_ge(s["qk_ready"], p + 1)
                if p:
                    pe.wait_ge(s["cx_ready"], p)
                for c in range(CHUNKS):
                    ins = mm(bank[2 + c // 16][:, 32 * (c % 16):32 * (c % 16) + 32], chunk(p, c),
                             qk_sb[:, :].rearrange("p (g w c j) -> p g c w j", g=4, w=2, c=8)[:, c // 8, c % 8])
                ins.then_inc(s["sT_ps"], 1)
                pe.wait_ge(s["sT_ready"], p + 1)
                for g in range(4):
                    ins = transpose(bank[5][:, 128 * g:128 * g + 128],
                                    sT_sb[:, 8 * g:8 * g + 8, :].rearrange("p c j -> p (c j)"), 128)
                ins.then_inc(s["sc_ps"], 1)
                if p + 1 < PAIRS:
                    x_blocks(p + 1)
                pe.wait_ge(s["probs"], p + 1)
                for g in range(4):
                    ins = transpose(bank[7][:, 128 * g:128 * g + 128],
                                    pr_sb[:, 2 * g:2 * g + 2, :].rearrange("p w k -> p (w k)"), 128)
                ins.then_inc(s["pT_ps"], 1)
                pe.wait_ge(s["pT_ready"], p + 1)
                pe.wait_ge(s["xT_ready"], 8 * (p + 1))
                for c in range(CHUNKS):
                    ins = mm(bank[2 + c // 16][:, 32 * (c % 16):32 * (c % 16) + 32],
                             xT[p % 2][:, 128 * c:128 * c + 128], pT_sb[:, c, :, :].rearrange("p w j -> p (w j)"))
                ins.then_inc(s["cx_ps"], 1)
                pe.wait_ge(s["cx_ready"], p + 1)
                mm(bank[4][:, :], wt("tok_WvT"), cx_sb[:, :, :].rearrange("p n h -> p (n h)")).then_inc(s["v_ps"], 1)
                pe.wait_ge(s["ctx_ready"], p + 1)
                mm(bank[6][:, 128:192], wt("tok_WoT"), ctx_sb[:, :]).then_inc(s["o_ps"], 1)
                pe.wait_ge(s["hT_ready"], p + 1)
                transpose(bank[6][0:64, 256:384], hT_sb[:, :], 128).then_inc(s["hn_ps"], 1)

            def u_blocks(r, src):
                for j in range(NPAIR):
                    ins = transpose(bank[j // 4][:, 128 * (j % 4):128 * (j % 4) + 128],
                                    src[:, 2 * j:2 * j + 2, :].rearrange("p i h -> p (i h)"), 128)
                ins.then_inc(s["uT_ps"], 1)

            def u(j):
                return uT[:, 128 * j:128 * j + 128]

            def project(w):
                for j in range(NPAIR):
                    ins = mm(bank[2 + j // 4][:, 128 * (j % 4):128 * (j % 4) + 128], u(j), w)
                return ins
            pe.wait_ge(s["u_ready"], 1)
            u_blocks(0, y1)
            pe.wait_ge(s["uTa_ready"], 1)
            pe.wait_ge(s["uTb_ready"], 1)
            pe.wait_ge(s["wssm_in"], 16)
            project(ws("WinT")).then_inc(s["lin_ps"], 1)
            pe.wait_ge(s["u_ready"], 2)
            u_blocks(1, hs)
            pe.wait_ge(s["mt_ready"], 4)
            pe.wait_ge(s["r_ready"], 4)
            for l in range(SSM_LAYERS):
                pe.wait_ge(s["uTa_ready"], l + 2)
                pe.wait_ge(s["uTb_ready"], l + 2)
                state = bank[5][0:64, 0:128].rearrange("p (b k) -> p b k", k=CK)
                for j in range(NPAIR):
                    ins = mm(bank[5][0:64, 0:128], WS[:, l, NPAIR - 1 - j, :], u(j), start=j == 0, stop=j == NPAIR - 1)
                ins.then_inc(s["f_ps"], 1)
                project(ws(f"DT{l}"))
                for j in range(NPAIR):
                    ins = mm(bank[4][:, 0:L], u(j), KZ[:, l, L - 1 - 2 * j:2 * L - 1 - 2 * j], start=j == 0, stop=False,
                             skip_group_check=True)
                for k, (m, X, by) in enumerate(((12, X0, 1), (24, X1, 2))):
                    pe.wait_ge(s["x_copied"], 2 * l + k + 1)
                    mm(state[:, :, by:CK], tra(m, l), X[:, :, 0:CK - by], start=False, stop=True, skip_group_check=True)\
                        .then_inc(s["f_ps"], 1)
                pe.wait_ge(s["xs_ready"], l + 1)
                for k in range(4):
                    ins = mm(bank[4][:, 0:L], XS[:, k, :, :].rearrange("p b k -> p (b k)"), R[:, l, k, :], start=False, stop=k == 3,
                             skip_group_check=True)
                ins.then_inc(s["c_ps"], 1)
                if l + 1 < SSM_LAYERS:
                    pe.wait_ge(s["u_ready"], l + 3)
                    u_blocks(l + 2, hs)
            pe.wait_ge(s["u_ready"], 3 + SSM_LAYERS)
            u_blocks(5, y1)
            pe.wait_ge(s["uTa_ready"], 6)
            pe.wait_ge(s["uTb_ready"], 6)
            project(ws("WoutT")).then_inc(s["wout_ps"], 1)

            pe.wait_ge(s["x2_ready"], 1)
            u_blocks(6, x2)
            pe.wait_ge(s["uTa_ready"], 7)
            pe.wait_ge(s["uTb_ready"], 7)
            pe.wait_ge(s["ffn_in"], 32)
            pe.wait_ge(s["h_ready"], 1)
            for g in range(4):
                par, mt = g // 2, g % 2
                q = slice(64 * par, 64 * par + 64)
                for k in range(2):
                    n = 512 if k == 0 else 256
                    if 2 * g + k >= 6:
                        pe.wait_ge(s["ff1_ready"], 2 * g + k - 5)
                    mm(bank[2 + (2 * g + k) % 6][:, 0:n], wf("w1")[q, 128 * mt:128 * mt + 128],
                       uT[q, 512 * k:512 * k + n]).then_inc(s["ff1_ps"], 1)
            pe.wait_ge(s["wexp_ready"], 1)
            mm(bank[1][:, 256:256 + T], wf("sameb"), w_all4[:, :, :].rearrange("p k i -> p (k i)"))
            mm(bank[1][:, 256 + T:256 + T + L], ident, tok_w[:, :]).then_inc(s["wall_ps"], 1)
            pe.wait_ge(s["ff1_ready"], 8)
            pe.wait_ge(s["wall_ready"], 1)
            for i in range(L):
                for mt in range(2):
                    ins = mm(bank[i // 8][:, 64 * (i % 8):64 * (i % 8) + 64],
                             G[:, mt, i % 2, 128 * (i // 2):128 * (i // 2) + 128],
                             wf("w2")[:, 64 * mt:64 * mt + 64], start=mt == 0, stop=mt == 1)
            ins.then_inc(s["ff2_ps"], 1)

            pe.wait_ge(s["x3_ready"], 1)
            pe.wait_ge(s["h2_ready"], 1)
            for i in range(L):
                ins = transpose(bank[i // 4][0:64, 128 * (i % 4):128 * (i % 4) + 128], x3[:, i, :], 128)
            ins.then_inc(s["xN_ps"], 1)
            pe.wait_ge(s["xN_ready"], 2)
            pe.wait_ge(s["late_in"], LATE)

            def tokens(b):
                return xN[:, b, :, :].rearrange("p k i -> p (k i)")

            def qk(b, which):
                if which:
                    pe.wait_ge(s["Q_ready"], b + 1)
                for m in range(2):
                    ins = mm(bank[0][:, T * m:T * m + T], w_att[:, which, m, :], tokens(b))
                ins.then_inc(s["QKV_ps"], 1)

            def value(b):
                pe.wait_ge(s["K_ready"], 2 * b + 2)
                for a in range(2):
                    ins = mm(bank[0][0:HALF, 2 * 128 * a:2 * 128 * a + 256], tokens(b)[:, HALF * a:HALF * a + HALF],
                             w_att[:, 2, :, :].rearrange("p m n -> p (m n)"))
                ins.then_inc(s["QKV_ps"], 1)
            qk(0, 0)
            qk(0, 1)
            value(0)
            pe.wait_ge(s["V_ready"], 1)
            pe.wait_ge(s["ones_set"], 2)
            for n in range(UNITS + 5):
                b, slot = divmod(n, 6)
                if n < UNITS:
                    heads, keys = unit_shape(n)
                    h0, a = unit_of(n)
                    if n >= 3:
                        pe.wait_ge(s["S_centered"], n - 2)
                    dst = bank[5 + n % 3][0:HALF, 0:UNIT]
                    mm(dst, identb[:, :], alibi[:, h0:h0 + heads, T - keys:T], start=True, stop=False, skip_group_check=True)
                    mm(dst, QT[:, b % 2, h0 // 4, HALF * a:HALF * a + HALF],
                       KT[:, b % 2, h0 // 4, h0 % 4:h0 % 4 + heads, 0:keys], start=False, stop=True,
                       skip_group_check=True).then_inc(s["S_ps"], 1)
                if b + 1 < B and slot in (0, 1):
                    if slot == 0 and b >= 2:
                        pe.wait_ge(s["h3_ready"], b - 1)
                    qk(b + 1, slot)
                if b + 1 < B and slot == 2:
                    value(b + 1)
                if b and slot == 3:
                    pe.wait_ge(s["o_ready"], b)
                    pe.wait_ge(s["V_ready"], min(b + 2, B))
                    for k in range(4):
                        ins = transpose(bank[0][:, HALF * k:HALF * k + HALF],
                                        o_n[:, k // 2, 4 * (k % 2):4 * (k % 2) + 4, :].rearrange("p h d -> p (h d)"), HALF)
                    ins.then_inc(s["oT_ps"], 1)
                if b and slot == 4:
                    pe.wait_ge(s["oT_ready"], b)
                    for a in range(2):
                        for k in range(2):
                            ins = mm(bank[0][0:HALF, D * a:D * a + D], oT[:, 2 * a + k, :], we("Wo")[:, D * k:D * k + D],
                                     start=k == 0, stop=k == 1)
                    ins.then_inc(s["wo_ps"], 1)
                if 1 <= n <= UNITS:
                    m = n - 1
                    pe.wait_ge(s["S_exped"], m + 1)
                    if m >= 2:
                        pe.wait_ge(s["PT_ready"], m - 1)
                    for k in range(4):
                        ins = transpose(bank[3 + m % 2][0:HALF, HALF * k:HALF * k + HALF],
                                        S[:, m % 3, HALF * k:HALF * k + HALF], HALF)
                    ins.then_inc(s["PT_ps"], 1)
                if 2 <= n < UNITS + 2:
                    m = n - 2
                    heads, keys = unit_shape(m)
                    h0, a = unit_of(m)
                    pe.wait_ge(s["PT_ready"], m + 1)
                    if m % 6 == 0 and m:
                        pe.wait_ge(s["o_ready"], m // 6)
                    parts = keys // HALF
                    for k in range(heads):
                        for c in range(parts):
                            at = HALF * (parts * k + c)
                            ins = mm(bank[1 + a][0:HALF, (AD + 1) * (h0 + k):(AD + 1) * (h0 + k + 1)],
                                     PT[:, m % 2, at:at + HALF], V[:, (m // 6) % 2, c, h0 + k, :],
                                     start=c == 0, stop=c == parts - 1)
                    ins.then_inc(s["PV_ps"], 1)

            pe.wait_ge(s["x4_ready"], 1)

            def blocks64(src, then):
                for i in range(L):
                    ins = transpose(bank[i // 4][0:64, 128 * (i % 4):128 * (i % 4) + 128], src[:, i, :], 128)
                ins.then_inc(s[then], 1)
            blocks64(x4, "x4T_ps")
            pe.wait_ge(s["x4T_ready"], 2)
            pe.wait_ge(s["late_in"], LATE)
            for i in range(L):
                ins = mm(bank[3 + i // 8][:, 64 * (i % 8):64 * (i % 8) + 64], x4T[:, 128 * i:128 * i + 128], we("Wr")[0:64, :])
            ins.then_inc(s["logits_ps"], 1)
            pe.wait_ge(s["oh_ready"], 1)
            for k in range(2):
                lo, hi = (0, 8) if k == 0 else (8, L)
                dst = bank[5 + k]
                mm(dst[:, 0:64 * (hi - lo)], wb("before"), OH[:, 2, lo:hi, :], start=True, stop=False, skip_group_check=True)
                for i in range(hi - 1):
                    a = max(lo, i + 1)
                    mm(dst[:, 64 * (a - lo):64 * (hi - lo)], wb("ones_b"),
                       OH[:, 2, i, :].unsqueeze(1).broadcast_to([128, hi - a, E]),
                       start=False, stop=i == hi - 2, skip_group_check=True)
            for i in range(L):
                ins = mm(bank[7][0:64, 0:1], OH[:, 2, i, :], wb("ones_b")[:, 0:1], start=i == 0, stop=i == L - 1)
            ins.then_inc(s["rank_ps"], 1)
            pe.wait_ge(s["nblk_ready"], 1)
            mm(bank[7][:, 64:128], n_bc[:, :], wm("before_e")[0:64, :])
            mm(bank[7][0:64, 1:2], wm("upto_e")[0:64, :], n_blk[:, :]).then_inc(s["base_ps"], 1)
            pe.wait_ge(s["nblk_ready"], 2)
            mm(bank[7][0:1, 128:128 + NBLK], wm("ones")[0:64, 0:1], blk_cmp[:, :]).then_inc(s["blke_ps"], 1)
            pe.wait_ge(s["cmb_ready"], 1)
            blocks64(y1, "cmbT_ps")
            pe.wait_ge(s["cmbT_ready"], 2)
            for i in range(L):
                ins = mm(bank[3 + i // 8][:, 64 * (i % 8):64 * (i % 8) + 64], x4T[:, 128 * i:128 * i + 128], wm("b2")[0:64, :])
            ins.then_inc(s["b2_ps"], 1)
            pe.wait_ge(s["b2_added"], 1)
            pe.wait_ge(s["moe_consts"], 1)
            with pe.Fori(0, GROUPS // 2) as pair:
                for u in range(2):
                    g = pair * 2 + u
                    pe.wait_ge(xg_in[u], pair * 16 + 16)
                    pe.sem_inc(s["xg_seen"], 1)
                    for q in range(GB // 2):
                        ins = transpose(bank[u][0:64, 128 * q:128 * q + 128], x_g[:, u, q, :], 128)
                    ins.then_inc(s["xT8_ps"], 1)
                    pe.wait_ge(s["xT8_ready"], g + 3)
                    pe.wait_ge(s["W8_ready"], g + 1)
                    for k in range(GB):
                        ins = mm(bank[2 + u][:, BLK * k:BLK * k + BLK], W_sb[0:D + 1, u, k, 0:EH],
                                 xT_sb[0:D + 1, u, BLK * k:BLK * k + BLK])
                    ins.then_inc(s["h8_ps"], 1)
                    pe.wait_ge(s["h8_ready"], g + 1)
                    pe.wait_ge(s["y8_ready"], g + 1)
                    for k in range(GB):
                        ins = mm(bank[4 + u][64 * (k % 2):64 * (k % 2) + 64, D * (k // 2):D * (k // 2) + D],
                                 h_sb[:, u, BLK * k:BLK * k + BLK], W_sb[:, u, k, EH:EW])
                    ins.then_inc(s["y8_ps"], 1)






def _pack(cols, parts, values):
    out = np.zeros((parts, sum(n for _, n in cols)), np.float32)
    at = 0
    for name, n in cols:
        v = values[name]
        out[:v.shape[0], at:at + n] = v
        at += n
    return out


def _diag2(m):
    out = np.zeros((128, 128), np.float32)
    out[:64, :64] = m
    out[64:, 64:] = m
    return out


def _twice(v):
    return np.concatenate([v, v], axis=0)


def _row(v, parts=128):
    return np.broadcast_to(np.reshape(v, (1, -1)), (parts, v.size))


def _layout(a):
    head = np.zeros((128, 2, NH), np.float32)
    for p in range(128):
        head[p, p // 64, (p % 64) // (D // NH)] = 1.0
    part = np.arange(128)
    f = {
        "w_tok": _pack(WTOK, 128, {
            "ident": np.eye(128, dtype=np.float32), "tok_WqT": _diag2(a["L0_tok_Wq"].T), "tok_Wk": _diag2(a["L0_tok_Wk"]),
            "tok_WvT": _diag2(a["L0_tok_Wv"].T), "tok_WoT": _diag2(a["L0_tok_Wo"].T),
            "tok_bq": _twice(a["L0_tok_bq"][:, None]), "tok_bk": _twice(a["L0_tok_bk"][:, None]),
            "tok_bv": _twice(a["L0_tok_bv"][:, None]), "tok_bo": _twice(a["L0_tok_bo"][:, None]),
            "headsel": head.reshape(128, 16), "headsel8": head[:, 0] + head[:, 1],
            "mean": np.full((128, 1), 1.0 / D, np.float32)}),
        "w_a": np.stack([_pack(WA, 64, {
            "A": a["L0_attn_A"][l], "AT": a["L0_attn_A"][l].T,
            "BB": np.concatenate([a["L0_attn_Bm"][l], a["L0_attn_Bm"][l]], axis=1), "C": a["L0_attn_Cm"][l]})
            for l in range(SSM_LAYERS)], axis=1),
        "w_ssm": _pack(WSSM, 128, {
            "WinT": _diag2(a["L0_attn_Win"].T), "bin": _row(a["L0_attn_bin_"]),
            "WoutT": _diag2(a["L0_attn_Wout"].T), "bout": _row(a["L0_attn_bout"]),
            **{f"DT{l}": _diag2(a["L0_attn_Dm"][l].T) for l in range(SSM_LAYERS)}}),
        "w_ffn": _pack(WFFN, 128, {
            "wr": _row(a["L0_ffn_wr"]), "br": _row(a["L0_ffn_br"]), "w1": _twice(a["L0_ffn_w1"]),
            "b1": a["L0_ffn_b1"].reshape(2, 128).T, "w2": a["L0_ffn_w2"].reshape(2, 128, D).transpose(1, 0, 2).reshape(128, 2 * D),
            "b2": _row(a["L0_ffn_b2"]),
            "sameb": (part[:, None] // CK == part[None, :] // CK).astype(np.float32),
            "isck": (part[:, None] % CK == np.arange(CK)[None, :]).astype(np.float32)}),
    }
    tok = (part % CK)[:, None] * L + np.arange(L)[None, :]
    f["earlier"] = (np.arange(T)[None, None, :] < tok[:, :, None]).astype(mybir.dt.np(BF16))
    f["w_att"] = np.concatenate([a["L1_attn_Wq"], a["L1_attn_Wk"], a["L1_attn_Wv"]], axis=1)
    f["w_exp"] = _pack(WEXP, 128, {
        "Wo": a["L1_attn_Wo"].reshape(2, 128, D).transpose(1, 0, 2).reshape(128, 2 * D), "bo": _row(a["L1_attn_bo"]),
        "Wr": a["L1_ffn_Wr"], "rbr": _row(a["L1_ffn_br"])})
    t, k = np.arange(HALF)[:, None] + HALF, np.arange(T)[None, :]
    slope = 0.5 ** np.arange(1, AH + 1)
    f["alibi"] = np.where((k <= t)[:, None, :], slope[None, :, None] * (k - t)[:, None, :], -1e30).astype(mybir.dt.np(BF16))
    f["identb"] = np.eye(HALF).astype(mybir.dt.np(BF16))
    e = np.arange(E)
    f["w_experts"] = np.zeros((128, E, EW), np.float32)
    f["w_experts"][0:D, :, 0:EH] = a["L1_ffn_W1"].transpose(1, 0, 2)
    f["w_experts"][D, :, 0:EH] = a["L1_ffn_b1"]
    f["w_experts"][:, :, EH:] = a["L1_ffn_W2"].transpose(1, 0, 2)
    f["w_moe"] = _pack(WMOE, 128, {
        "b2": a["L1_ffn_b2"], "before_e": BLK * (e[:, None] < e[None, :]), "upto_e": (e[:, None] <= e[None, :]),
        "iota_m": _row(np.arange(NBLK)), "steps": _row(BLK * np.arange(TOK // BLK)), "ones": np.ones((128, 128))})
    f["w_bit"] = np.concatenate([part[:, None] < part[None, :], np.ones((128, 128)), _row(e)], axis=1).astype(mybir.dt.np(BF16))
    return f


def kernel(**inputs):
    import concourse.bacc as _bacc
    from concourse.bass_utils import run_bass_kernel_spmd as _run

    a = {k: np.asarray(v) for k, v in inputs.items()}
    nc = _bacc.Bacc("TRN2", target_bir_lowering=False, num_devices=1)
    feeds = {"x": a["x"], "txt": a["txt"], **_layout(a)}
    arrays, args = {}, {}
    for name, v in feeds.items():
        v = np.ascontiguousarray(v)
        arrays[f"in_{name}"] = v
        args[name] = nc.dram_tensor(f"in_{name}", v.shape, mybir.dt.from_np(v.dtype), kind="ExternalInput").ap()
    out = nc.dram_tensor("out_0", (B, T, D), F32, kind="ExternalOutput").ap()
    build(nc, args, out)
    r = _run(nc, [arrays], core_ids=[0])
    return r.results[0]["out_0"]
```

```python
import numpy as np
import concourse.bass as bass
from concourse import mybir
from contextlib import ExitStack

F32 = mybir.dt.float32
BF16 = mybir.dt.bfloat16
I32 = mybir.dt.int32
U32 = mybir.dt.uint32
ALU = mybir.AluOpType
ACT = mybir.ActivationFunctionType
AX = mybir.AxisListType

B, D, IMG = 8, 64, 64
GS, NH = 8, 8
WIN = (IMG // GS) ** 2
KWIN = GS * GS
TXT = 128
T = WIN + TXT
TOK = B * T
PAIRS = B // 2
POOL_ROWS = 5
WARM_UP = 5
CHUNKS = WIN // 2
CK = 16
L = T // CK
NPAIR = L // 2
SSM_LAYERS = 4
EPS = 1e-5
HID = 4 * D
CAP = T // 2 - 1
AH, AD = 8, 32
HALF = T // 2
TILES = TOK // HALF
UNIT = 4 * HALF
UNITS = 6 * B
E, EH = 64, 128
EW = EH + D
BLK = 64
NBLK = (2 * TOK + E * (BLK - 1)) // BLK // 8 * 8 + 8
GB = 8
GROUPS = NBLK // GB
SLOTS = NBLK * BLK

WTOK = [("ident", 128), ("tok_WqT", 128), ("tok_Wk", 128), ("tok_WvT", 128), ("tok_WoT", 128),
        ("tok_bq", 1), ("tok_bk", 1), ("tok_bv", 1), ("tok_bo", 1), ("headsel", 16), ("headsel8", 8), ("mean", 1)]
WA = [("A", 64), ("AT", 64), ("BB", 128), ("C", 64)]
WSSM = [("WinT", 128), ("bin", 64), ("WoutT", 128), ("bout", 64)] + [(f"DT{l}", 128) for l in range(SSM_LAYERS)]
WFFN = [("wr", 64), ("br", 1), ("w1", HID), ("b1", 2), ("w2", 128), ("b2", 64), ("sameb", 128), ("isck", CK)]

WEXP = [("Wo", 2 * D), ("bo", D), ("Wr", E), ("rbr", E)]

WMOE = [("b2", D), ("before_e", E), ("upto_e", E), ("iota_m", NBLK), ("steps", TOK // BLK), ("ones", 128)]
WBIT = [("before", 128), ("ones_b", 128), ("iota_e", E)]


def offsets(cols):
    at, out = 0, {}
    for name, n in cols:
        out[name] = (at, n)
        at += n
    return out, at


def build(nc, d, out):
    with ExitStack() as ctx:
        def sb(name, shape, dt=F32):
            return ctx.enter_context(nc.sbuf_tensor(name, shape, dt))

        def sem(name):
            return ctx.enter_context(nc.semaphore(name))

        def packed(name, cols, parts=128):
            at, n = offsets(cols)
            t = sb("w_" + name, [parts, n])
            return t, (lambda key: t[:, at[key][0]:at[key][0] + at[key][1]])

        bank = [ctx.enter_context(nc.psum_tensor(f"bank{i}", [128, 512], F32)) for i in range(8)]
        img_tok = nc.dram_tensor("tokens_in", (B, T, D), F32, kind="Internal").ap()

        w_tok, wt = packed("tok", WTOK)
        w_ssm, ws = packed("ssm", WSSM)
        w_ffn, wf = packed("ffn", WFFN)
        w_a = sb("w_a", [64, SSM_LAYERS, offsets(WA)[1]])
        ident = wt("ident")

        def wa(key, l):
            at, n = offsets(WA)[0][key]
            return w_a[:, l, at:at + n]

        big = sb("big", [128, 3 * IMG * IMG])
        pixels = [big[:, IMG * IMG * u:IMG * IMG * (u + 1)] for u in range(3)]
        xw = [sb(f"windows{u}", [128, WIN, KWIN]) for u in range(2)]
        xT = [sb(f"xT{u}", [128, CHUNKS * 128]) for u in range(2)]
        q_sum = sb("q_sum", [128, WIN])
        q_mean = sb("q_mean", [128, PAIRS, WIN])
        HEADS = 16 * WIN + 16
        head_buf = sb("head_buf", [128, 2 * HEADS + 512 + 1024])
        q_head = head_buf[:, 0:16 * WIN].rearrange("p (n j) -> p n j", j=16)
        qk_sb = head_buf[:, HEADS:2 * HEADS]
        qb_sb = sb("qb_sb", [128, 16])
        sc_sb = sb("sc_sb", [128, 16, KWIN])
        mx_sb = sb("mx_sb", [128, 16])
        sm_sb = sb("sm_sb", [128, 16])
        pT_sb = sb("pT_sb", [128, CHUNKS, 2, 16])
        cx_sb = head_buf[:, 2 * HEADS:2 * HEADS + 512].rearrange("p (n h) -> p n h", h=8)
        raw_sb = head_buf[:, 2 * HEADS + 512:2 * HEADS + 1536]
        vm_sb = raw_sb[:, 0:512].rearrange("p (n h) -> p n h", h=8)
        ctx_sb = sb("ctx_sb", [128, WIN])
        hT_sb = sb("hT_sb", [128, WIN])
        hn_sb = sb("hn_sb", [64, PAIRS, 128])

        Z = sb("Z", [64, SSM_LAYERS, L, 65])
        pw = sb("pw", [64, 6, SSM_LAYERS, 2, 64])
        R = sb("R", [64, SSM_LAYERS, 4, L])
        KZ = sb("KZ", [128, SSM_LAYERS, 2 * L])
        WS = sb("WS", [128, SSM_LAYERS, NPAIR, 64])

        areas = [big[:, :]] + [t[:, :] for t in xT] + [t[:, :, :].rearrange("p n k -> p (n k)") for t in xw] + [head_buf[:, :]]
        taken = [0] * len(areas)

        def over(p, shape, dt=F32):
            n = int(np.prod(shape[1:])) * (2 if dt == BF16 else 4) // 4
            v = areas[p][0:shape[0], taken[p]:taken[p] + n]
            taken[p] += n
            assert taken[p] <= areas[p].shape[1]
            if dt != F32:
                v = v.bitcast(dt)
            names = "abcd"[:len(shape) - 1]
            return v.rearrange(f"p ({' '.join(names)}) -> p {' '.join(names)}", **dict(zip(names, shape[1:])))

        hL = sb("hL", [128, L, D])
        xc = over(1, [128, L, D])
        sq = over(1, [128, L, D])
        y1 = over(1, [128, L, D])
        hs = over(1, [128, L, D])
        uT = over(1, [128, NPAIR * 128])
        ln_s = sb("ln_s", [128, L])
        ln_m = sb("ln_m", [128, L])
        ln_q = sb("ln_q", [128, L])
        ln_v = sb("ln_v", [128, L])
        rstd = sb("rstd", [128, L])
        mhalf = sb("mhalf", [128, 16])
        c_sb = sb("c_sb", [128, L])
        X0 = sb("X0", [64, B, CK])
        X1 = sb("X1", [64, B, CK])
        XS = sb("XS", [64, 4, B, CK])

        x2 = over(0, [128, L, D])
        G = over(0, [128, 2, 2, NPAIR * 128])
        tok_w = over(0, [128, L])
        w_all4 = over(0, [128, CK, L])
        w_all = over(0, [128, T + L])
        ahead = over(0, [128, L, T], BF16)
        tied = over(0, [128, L, T], BF16)
        earlier = sb("earlier", [128, L, T], BF16)
        rank = over(0, [128, L])
        w_sel = over(0, [128, L])

        w_att = over(2, [64, 3, 2, 128])
        w_exp = sb("w_exp", [128, offsets(WEXP)[1]])
        x3 = over(2, [128, L, D])
        xN = over(2, [64, B, CK, L])
        alibi = over(4, [HALF, AH, T], BF16)
        identb = over(4, [HALF, HALF], BF16)
        QT = over(3, [128, 2, 2, T])
        KT = over(3, [128, 2, 2, 4, T])
        V = over(4, [HALF, 2, 2, AH, AD + 1])
        S = over(5, [HALF, 3, UNIT])
        S_max = over(1, [HALF, 3, 4])
        PT = over(4, [HALF, 2, UNIT])
        o_inv = over(1, [HALF, 2, AH])
        o_n = over(2, [HALF, 2, AH, AD])
        oT = over(5, [128, 4, HALF])
        hN = over(5, [HALF, TILES, D])

        taken[2] = taken[3] = taken[4] = 0
        W_all = big[:, :].rearrange("p (e n) -> p e n", n=EW)
        x_slots = nc.dram_tensor("x_slots", (SLOTS, D), F32, kind="Internal").ap()
        y_slots = nc.dram_tensor("y_slots", (SLOTS, D), F32, kind="Internal").ap()
        w_moe, wm = packed("moe", WMOE)
        w_bit = sb("w_bit", [128, offsets(WBIT)[1]], BF16)
        zero = sb("zero", [128, D])
        x4T = over(2, [64, L * 128])
        x4 = over(2, [128, L, D])
        logits = over(2, [128, L, E])
        top = sb("top", [128, L, 8])
        top_e = sb("top_e", [128, L, 8], U32)
        top_b = sb("top_b", [128, L, 2], BF16)
        W_sb = over(3, [128, 2, GB, EW])
        xT_sb = over(3, [EH, 2, GB * BLK])
        h_sb = over(2, [EH, 2, GB * BLK])
        x_g = over(4, [128, 2, GB // 2, D])
        y_g = over(4, [128, 2, GB // 2, D])
        OH = over(4, [128, 3, L, E], BF16)
        y_back = over(4, [128, 2, L, D])
        gate = sb("gate", [128, 4, L])
        n_blk = sb("n_blk", [64, 1])
        blk_cmp = sb("blk_cmp", [64, NBLK])
        n_bc = sb("n_bc", [64, 128])
        base = sb("base", [128, E])
        end = sb("end", [64, 1])
        slot_f = sb("slot_f", [128, 2, L])
        slot_i = sb("slot_i", [128, 3, 2, L], I32)
        addr = sb("addr", [128, 2, L], U32)
        blk_e = sb("blk_e", [1, NBLK], I32)

        def wb(key):
            at, n = offsets(WBIT)[0][key]
            return w_bit[:, at:at + n]

        def we(key):
            at, n = offsets(WEXP)[0][key]
            return w_exp[:, at:at + n]

        s = {n: sem(n) for n in """wssm_in txt_in consts_set dve_own cbar_ps pow_ps pow_ready z_ps z_ready mt_ps mt_ready r_ready pads_set raw_ready turned_ps
            xw_pool_ready xw_act_ready q_ready qp_ps qhead_ready qk_ps qk_ready qb_ready xT_ps xT_ready s_ps centered
            exped probs pT_ps pT_ready cx_ps cx_ready v_ps ctx_ready o_ps hT_ready hn_ps hn_ready ln_centered
            ln_squared ln_var ln_rstd u_ready uT_ps uTa_ready uTb_ready lin_ps f_ps x_copied xs_ready c_ps y_ready
            gelu_ready hLb_ready wout_ps h_ready ff1_ps ff1_ready ff2_ps wexp_ready wall_ps wall_ready x3_ready xN_ps
            xN_ready ones_set hb_ready x4_ready x4T_ps x4T_ready logits_ps top_gap oh_ready rank_ps nblk_ready
            base_ps addr_ready blke_ps blke_ready gap_exped cmb_ready cmbT_ps cmbT_ready b2_ps b2_added zero_set
            slots_zeroed wall_in xg_seen xT8_ps xT8_ready W8_ready h8_ps h8_ready y8_ps y8_ready 
            moe_consts QKV_ps Q_ready K_ready V_ready S_ps S_centered S_exped PT_ps PT_ready PV_ps o_ready oT_ps
            oT_ready wo_ps h3_ready x2_ready hx_ready h2_ready out_done ffn_in first_in late_in res_in res_out""".split()}
        scattered = [sem(f"scattered{k}") for k in range(6)]
        gathered = [sem(f"gathered{k}") for k in range(6)]
        xg_in = [sem(f"xg_in{k}") for k in range(2)]
        y8_out = [sem(f"y8_out{k}") for k in range(2)]
        s["y_stored"], s["out_ready"] = sem("y_stored"), sem("out_ready")
        xs = [sem(f"pixels{p}_in") for p in range(PAIRS)]
        LATE = 16 * 6
        LEVELS = [(2, 1, 1), (4, 2, 2), (8, 4, 4), (12, 8, 4), (24, 12, 12), (48, 24, 24)]
        AT = {m: i for i, (m, _, _) in enumerate(LEVELS)}
        WROW = 2 * L

        def nat(m, l):
            return wa("A", l) if m == 1 else pw[:, AT[m], l, 0, :]

        def tra(m, l):
            return wa("AT", l) if m == 1 else pw[:, AT[m], l, 1, :]

        def flat(t):
            return t[:, :, :].rearrange("p i h -> p (i h)")

        def half_bank(t, k):
            return t[:, 0:8, :] if k == 0 else t[:, 8:L, :]

        def bank_tokens(k, two):
            n = 8 if k == 0 else L - 8
            return bank[two + k][:, 0:64 * n].rearrange("p (i h) -> p i h", h=D)

        def sort_row(copy, p, gw):
            return copy(xw[p % 2][:, 8 * gw:8 * gw + 8, :].rearrange("p gh (r s) -> p gh r s", r=GS),
                        pixels[p % 3][:, 512 * gw:512 * gw + 512].rearrange("p (r gh s) -> p gh r s", r=GS, gh=8))

        def rows(k):
            return 8 if k == 0 else L - 8

        def unit_shape(n):
            return (4, HALF) if n % 3 == 0 else (2, T)

        def unit_of(n):
            slot = n % 6
            return 4 * (slot // 3) + (0, 0, 2)[slot % 3], int(slot % 3 > 0)

        def tokens_of(k):
            return xN[:, :, :, 4 * k:4 * k + 4].rearrange("p b k i -> p (b k) i")

        block = ctx.enter_context(nc.Block())

        @block.sync
        def _(sp):
            sp.dma_start(w_tok[:, :], d["w_tok"]).then_inc(s["first_in"], 16)
            sp.dma_start(w_a[:, :, :], d["w_a"]).then_inc(s["first_in"], 16)
            for p in range(PAIRS):
                if p >= 3:
                    sp.wait_ge(s["xw_pool_ready"], POOL_ROWS * (p - 2))
                    sp.wait_ge(s["xw_act_ready"], (8 - POOL_ROWS) * (p - 2))
                    sp.wait_ge(s["q_ready"], p - 2)
                sp.dma_start(pixels[p % 3][:, :], d["x"][2 * p:2 * p + 2].rearrange("b c w h -> (b c) (w h)"))\
                    .then_inc(xs[p], 16)
            sp.dma_start(img_tok[:, WIN:T, :], d["txt"]).then_inc(s["txt_in"], 16)
            sp.dma_start(w_ssm[:, :], d["w_ssm"]).then_inc(s["wssm_in"], 16)
            sp.dma_start(w_ffn[:, :], d["w_ffn"]).then_inc(s["ffn_in"], 16)
            sp.dma_start(earlier[:, :, :], d["earlier"]).then_inc(s["ffn_in"], 16)
            for p in range(PAIRS):
                sp.wait_ge(s["hn_ready"], p + 1)
                sp.dma_start(img_tok[2 * p:2 * p + 2, 0:WIN, :].rearrange("b n c -> n b c"),
                             hn_sb[:, p, :].rearrange("n (b c) -> n b c", b=2)).then_inc(s["res_out"], 16)
            sp.wait_ge(s["res_out"], 16 * PAIRS)
            sp.wait_ge(s["txt_in"], 16)
            sp.dma_start(flat(hL), img_tok.rearrange("b (k i) h -> (b k) (i h)", i=L)).then_inc(s["res_in"], 16)
            sp.wait_ge(s["hn_ready"], PAIRS)
            sp.dma_start(w_att[:, :, :, :].rearrange("p a b n -> p (a b n)"), d["w_att"]).then_inc(s["late_in"], 16)
            sp.dma_start(w_exp[:, :], d["w_exp"]).then_inc(s["late_in"], 16)
            sp.dma_start(alibi[:, :, :], d["alibi"]).then_inc(s["late_in"], 16)
            sp.dma_start(identb[:, :], d["identb"]).then_inc(s["late_in"], 16)
            sp.dma_start(w_moe[:, :], d["w_moe"]).then_inc(s["late_in"], 16)
            sp.dma_start(w_bit[:, :], d["w_bit"]).then_inc(s["late_in"], 16)
            sp.wait_ge(s["zero_set"], 1)
            sp.dma_start(x_slots.rearrange("(p q) h -> p q h", p=128),
                         zero[:, :].unsqueeze(1).broadcast_to([128, SLOTS // 128, D])).then_inc(s["slots_zeroed"], 16)
            sp.wait_ge(s["h2_ready"], 1)
            sp.dma_start(img_tok.rearrange("b (k i) h -> (b k) (i h)", i=L), flat(hL)).then_inc(s["res_out"], 16)
            sp.wait_ge(s["res_out"], 16 * (PAIRS + 1))
            sp.dma_start(hN[:, :, :], img_tok.rearrange("b (a t) h -> t (b a) h", t=HALF)).then_inc(s["res_in"], 16)
            sp.dma_start(W_all, d["w_experts"]).then_inc(s["wall_in"], 16)
            for b in range(B):
                sp.wait_ge(s["h3_ready"], b + 1)
                sp.dma_start(img_tok[b].rearrange("(a t) h -> t a h", t=HALF), hN[:, 2 * b:2 * b + 2, :]).then_inc(s["res_out"], 16)
            sp.wait_ge(s["res_out"], 16 * (PAIRS + 1 + B))
            sp.dma_start(flat(hL), img_tok.rearrange("b (k i) h -> (b k) (i h)", i=L)).then_inc(s["res_in"], 16)
            for k in range(6):
                sp.wait_ge(scattered[k], 16 * 4)
            xin = x_slots.rearrange("(p q) h -> p q h", p=128)
            yout = y_slots.rearrange("(p q) h -> p q h", p=128)
            with sp.Fori(0, GROUPS // 2) as pair:
                for u in range(2):
                    sp.wait_ge(s["xT8_ready"], pair * 2 + u + 1)
                    sp.dma_start(x_g[:, u, :, :], xin[:, bass.ds((pair * 2 + u) * (GB // 2), GB // 2), :]).then_inc(xg_in[u], 16)
            for k in range(2):
                sp.wait_ge(y8_out[k], 16 * (GROUPS // 2 + 1))
            sp.sem_inc(s["y_stored"], 1)
            for k in range(2):
                sp.wait_ge(s["out_ready"], k + 1)
                sp.dma_start(out.rearrange("b (k i) h -> (b k) i h", i=L)[:, 6 * k:6 * k + 6, :],
                             hL[:, 6 * k:6 * k + 6, :]).then_inc(s["out_done"], 16)
            sp.wait_ge(s["out_done"], 32)

        @block.gpsimd
        def _(pool):
            pool.memset(zero[:, :], 0.0).then_inc(s["zero_set"], 1)
            for k in (1, 2):
                pool.memset(head_buf[:, k * HEADS - 16:k * HEADS], 0.0).then_inc(s["pads_set"], 1)
            pool.memset(pT_sb[:, :, :, :], 0.0).then_inc(s["consts_set"], 1)
            pool.memset(KZ[:, :, :], 0.0).then_inc(s["consts_set"], 1)
            pool.memset(XS[:, :, :, :], 0.0).then_inc(s["consts_set"], 1)
            pool.memset(mhalf[:, :], -0.5).then_inc(s["consts_set"], 1)
            for p in range(PAIRS):
                pool.wait_ge(xs[p], 16)
                if p >= 2:
                    pool.wait_ge(s["s_ps"], p - 1)
                    pool.wait_ge(s["xT_ps"], 8 * (p - 1))
                for gw in range(POOL_ROWS):
                    sort_row(pool.tensor_copy, p, gw).then_inc(s["xw_pool_ready"], 1)
            pool.wait_ge(s["consts_set"], 4)

            def inv_std(n):
                pool.wait_ge(s["ln_var"], n + 1)
                pool.tensor_tensor(rstd[:, :], ln_v[:, :], mhalf[:, 0:L], ALU.pow).then_inc(s["ln_rstd"], 1)
            inv_std(0)
            pool.wait_ge(s["ln_centered"], 1)
            pool.wait_ge(s["wssm_in"], 16)
            pool.tensor_tensor(flat(hL).rearrange("p (i h) -> p i h", h=D), hL[:, :, :],
                               ws("bout").unsqueeze(1).broadcast_to([128, L, D]), ALU.add).then_inc(s["hLb_ready"], 1)
            for n in range(1, 6):
                inv_std(n)
            inv_std(6)
            pool.wait_ge(s["x2_ready"], 1)
            pool.tensor_tensor(hs[:, :, :], hL[:, :, :], x2[:, :, :], ALU.add).then_inc(s["hx_ready"], 1)
            inv_std(7)
            pool.memset(KT[:, :, :, :, :], 0.0).then_inc(s["ones_set"], 1)
            pool.memset(V[:, :, :, :, AD:AD + 1], 1.0).then_inc(s["ones_set"], 1)
            pool.wait_ge(s["res_in"], 32)
            pool.wait_ge(s["late_in"], LATE)
            pool.tensor_tensor(hN[:, :, :], hN[:, :, :], we("bo")[0:HALF, :].unsqueeze(1).broadcast_to([HALF, TILES, D]),
                               ALU.add).then_inc(s["hb_ready"], 1)
            inv_std(8)
            pool.wait_ge(s["h3_ready"], B)
            pool.wait_ge(s["ln_rstd"], 9)
            pool.memset(xT_sb[64:65, :, :], 1.0).then_inc(s["moe_consts"], 1)
            pool.wait_ge(s["slots_zeroed"], 16)
            pool.wait_ge(s["addr_ready"], 1)
            for k in range(2):
                for i in range(L):
                    pool.indirect_dma_start(x_slots, bass.IndirectOffsetOnAxis(addr[:, k, i:i + 1], 0), x4[:, i, :], None)\
                        .then_inc(scattered[(12 * k + i) // 4], 16)
            pool.wait_ge(s["y_stored"], 1)
            for i in range(L):
                for k in range(2):
                    pool.indirect_dma_start(y_back[:, k, i, :], None, y_slots, bass.IndirectOffsetOnAxis(addr[:, k, i:i + 1], 0))\
                        .then_inc(gathered[i // 2], 16)

        @block.scalar
        def _(act):
            copy = nc.scalar.copy

            def powers(n):
                act.wait_ge(s["pow_ps"], n + 1)
                copy(pw[:, n, :, :, :].rearrange("p l a n -> p (l a n)"), bank[0][0:64, :]).then_inc(s["pow_ready"], 1)

            def sort(p):
                act.wait_ge(xs[p], 16)
                if p >= 2:
                    act.wait_ge(s["s_ps"], p - 1)
                    act.wait_ge(s["xT_ps"], 8 * (p - 1))
                for gw in range(POOL_ROWS, 8):
                    sort_row(copy, p, gw).then_inc(s["xw_act_ready"], 1)

            def x_blocks(p, blocks):
                if p >= 2:
                    act.wait_ge(s["cx_ps"], p - 1)
                for g in blocks:
                    act.wait_ge(s["xT_ps"], 8 * p + g + 1)
                    copy(xT[p % 2][:, 512 * g:512 * g + 512], bank[g % 2][:, :]).then_inc(s["xT_ready"], 1)

            def keyed_queries(p):
                act.wait_ge(s["qk_ps"], p + 1)
                if p:
                    act.wait_ge(s["s_ps"], p)
                copy(qk_sb[:, 0:512], bank[4][:, :])
                copy(qk_sb[:, 512:1024], bank[5][:, :]).then_inc(s["qk_ready"], 1)

            def exponentials(p):
                act.wait_ge(s["centered"], p + 1)
                nc.scalar.activation(sc_sb[:, :, :], sc_sb[:, :, :], ACT.Exp, scale=float(D // NH) ** -0.5)\
                    .then_inc(s["exped"], 1)

            def weighted_pixels(p):
                act.wait_ge(s["cx_ps"], p + 1)
                for k in range(2):
                    last = copy(raw_sb[:, 512 * k:512 * k + 512], bank[4 + k][:, :])
                last.then_inc(s["raw_ready"], 1)

            def weighted_channels(p):
                act.wait_ge(s["turned_ps"], p + 1)
                if p:
                    act.wait_ge(s["v_ps"], p)
                for b in range(2):
                    for k in range(2):
                        last = copy(cx_sb[64 * b:64 * b + 64, 32 * k:32 * k + 32, :],
                                    bank[4 + k][64 * b:64 * b + 64, :].rearrange("p (n b h) -> p n b h", b=2, h=8)[:, :, b, :])
                last.then_inc(s["cx_ready"], 1)

            def tokens_out(p):
                act.wait_ge(s["hn_ps"], p + 1)
                copy(hn_sb[:, p, :], bank[7][0:64, 64:192]).then_inc(s["hn_ready"], 1)
            def scan_matrices(l):
                act.wait_ge(s["mt_ps"], l + 1)
                act.wait_ge(s["consts_set"], 4)
                for half in range(2):
                    q = slice(64 * half, 64 * half + 64)
                    odd = 1 - half
                    copy(WS[q, l, 0:4, :], bank[0][q, :].rearrange("p (j a n) -> p j a n", a=2, n=64)[:, :, odd, :])
                    copy(WS[q, l, 4:6, :], bank[1][q, 0:256].rearrange("p (j a n) -> p j a n", a=2, n=64)[:, :, odd, :])
                    ins = copy(KZ[q, l, L + half:2 * L - 1 + half], bank[1][q, 256:256 + L - 1])
                if l:
                    ins = copy(R[:, :, l, :], bank[1][0:64, 320:320 + SSM_LAYERS * L].rearrange("p (m j) -> p m j", j=L))
                    ins.then_inc(s["r_ready"], 1)
                else:
                    ins.then_inc(s["mt_ready"], 1)

            for n in range(4):
                powers(n)
            sort(0)
            powers(4)
            powers(5)
            keyed_queries(0)
            x_blocks(0, range(4))
            sort(1)
            x_blocks(0, range(4, 8))
            scan_matrices(0)
            exponentials(0)
            for p in range(PAIRS):
                if p + 1 < PAIRS:
                    keyed_queries(p + 1)
                    x_blocks(p + 1, range(4))
                if p + 2 < PAIRS:
                    sort(p + 2)
                if p:
                    tokens_out(p - 1)
                weighted_pixels(p)
                if p + 1 < PAIRS:
                    x_blocks(p + 1, range(4, 6))
                if p + 1 < PAIRS:
                    exponentials(p + 1)
                weighted_channels(p)
                if p + 1 < PAIRS:
                    x_blocks(p + 1, range(6, 8))
                    scan_matrices(p + 1)
            tokens_out(PAIRS - 1)

            def squares(n, src):
                act.wait_ge(s["ln_centered"], n + 1)
                nc.scalar.activation(sq[:, :, :], src, ACT.Square).then_inc(s["ln_squared"], 1)

            def u_blocks(r):
                act.wait_ge(s["uT_ps"], r + 1)
                copy(uT[:, 0:512], bank[0][:, :]).then_inc(s["uTa_ready"], 1)
            squares(0, xc[:, :, :])
            u_blocks(0)
            u_blocks(1)
            for l in range(SSM_LAYERS):
                act.wait_ge(s["y_ready"], l + 1)
                nc.scalar.activation(sq[:, :, :], y1[:, :, :], ACT.Gelu).then_inc(s["gelu_ready"], 1)
                squares(l + 1, xc[:, :, :])
                if l + 1 < SSM_LAYERS:
                    u_blocks(l + 2)
            squares(5, xc[:, :, :])
            u_blocks(5)
            squares(6, xc[:, :, :])
            u_blocks(6)
            for g in range(4):
                par, mt = g // 2, g % 2
                for k in range(2):
                    n = 512 if k == 0 else 256
                    act.wait_ge(s["ff1_ps"], 2 * g + k + 1)
                    nc.scalar.activation(G[:, mt, par, 512 * k:512 * k + n], bank[2 + (2 * g + k) % 6][:, 0:n],
                                         ACT.Gelu_apprx_tanh, bias=wf("b1")[:, mt:mt + 1]).then_inc(s["ff1_ready"], 1)

            squares(7, xc[:, :, :])
            act.wait_ge(s["xN_ps"], 1)
            for k in range(2):
                ins = copy(tokens_of(k), bank[k][0:64, :].rearrange("p (i t) -> p t i", i=4))
            ins.then_inc(s["xN_ready"], 1)

            def query(b):
                act.wait_ge(s["QKV_ps"], 3 * b + 1)
                nc.scalar.activation(QT[:, b % 2, :, :].rearrange("p m t -> p (m t)"), bank[0][:, 0:2 * T], ACT.Copy,
                                     scale=float(AD) ** -0.5).then_inc(s["Q_ready"], 1)

            def key(b):
                act.wait_ge(s["QKV_ps"], 3 * b + 2)
                for k in (2, 3):
                    q = slice(AD * k, AD * k + AD)
                    ins = copy(KT[q, b % 2, :, k, :], bank[0][q, 0:2 * T].rearrange("p (m t) -> p m t", m=2))
                ins.then_inc(s["K_ready"], 1)
            query(0)
            act.wait_ge(s["ones_set"], 2)
            key(0)
            for n in range(UNITS + 4):
                b, slot = divmod(n, 6)
                if n < UNITS:
                    act.wait_ge(s["S_centered"], n + 1)
                    nc.scalar.activation(S[:, n % 3, :], S[:, n % 3, :], ACT.Exp).then_inc(s["S_exped"], 1)
                if b + 1 < B and slot == 0:
                    query(b + 1)
                if b + 1 < B and slot == 1:
                    key(b + 1)
                if b and slot == 3:
                    act.wait_ge(s["oT_ps"], b)
                    copy(oT[:, :, :].rearrange("p a t -> p (a t)"), bank[0][:, 0:4 * HALF]).then_inc(s["oT_ready"], 1)
                if 1 <= n <= UNITS:
                    act.wait_ge(s["PT_ps"], n)
                    if n >= 3:
                        act.wait_ge(s["PV_ps"], n - 2)
                    copy(PT[:, (n - 1) % 2, :], bank[3 + (n - 1) % 2][0:HALF, 0:UNIT]).then_inc(s["PT_ready"], 1)

            squares(8, xc[:, :, :])
            act.wait_ge(s["x4T_ps"], 1)
            for k in range(2):
                ins = copy(x4T[:, 512 * k:512 * k + 512], bank[k][0:64, :])
            ins.then_inc(s["x4T_ready"], 1)
            act.wait_ge(s["top_gap"], 1)
            nc.scalar.activation(gate[:, 1, :], gate[:, 0, :], ACT.Exp).then_inc(s["gap_exped"], 1)
            act.wait_ge(s["cmbT_ps"], 1)
            for k in range(2):
                ins = copy(x4T[:, 512 * k:512 * k + 512], bank[k][0:64, :])
            ins.then_inc(s["cmbT_ready"], 1)
            act.wait_ge(s["moe_consts"], 1)
            act.wait_ge(s["b2_ps"], 1)
            act.sem_inc(s["xT8_ready"], 2)
            with act.Fori(0, GROUPS // 2) as pair:
                for u in range(2):
                    g = pair * 2 + u
                    act.wait_ge(s["xT8_ps"], g + 1)
                    copy(xT_sb[0:64, u, :], bank[u][0:64, :]).then_inc(s["xT8_ready"], 1)
                    act.wait_ge(s["h8_ps"], g + 1)
                    nc.scalar.activation(h_sb[:, u, :], bank[2 + u][:, :], ACT.Relu).then_inc(s["h8_ready"], 1)
                    act.wait_ge(s["y8_ready"], g + 3)
                    act.dma_start(y_slots.rearrange("(p q) h -> p q h", p=128)[:, bass.ds(g * (GB // 2), GB // 2), :],
                                  y_g[:, u, :, :]).then_inc(y8_out[u], 16)

        @block.vector
        def _(dve):
            done = [0]

            def link(ins):
                done[0] += 1
                ins.then_inc(s["dve_own"], 1)
                dve.wait_ge(s["dve_own"], done[0])
            tt, ts = nc.vector.tensor_tensor, nc.vector.tensor_scalar
            copy, red = nc.vector.tensor_copy, nc.vector.tensor_reduce

            dve.wait_ge(s["first_in"], 32)
            for l in range(SSM_LAYERS):
                copy(Z[:, l, 0, 0:64], ident[0:64, 0:64])
            dve.wait_ge(s["cbar_ps"], 1)
            copy(Z[:, :, 0, 64], bank[7][0:64, 0:SSM_LAYERS]).then_inc(s["z_ready"], 1)
            for n, m in enumerate((1, 2, 4, 8)):
                k = min(m, L - m)
                dve.wait_ge(s["z_ps"], n + 1)
                for l in range(SSM_LAYERS):
                    ins = copy(Z[:, l, m:m + k, :], bank[1 + l][0:64, 0:65 * k].rearrange("p (j n) -> p j n", n=65))
                ins.then_inc(s["z_ready"], 1)
            dve.wait_ge(s["z_ready"], 5)
            copy(R[:, :, 0, :], Z[:, :, :, 64]).then_inc(s["r_ready"], 1)

            def means(p):
                dve.wait_ge(xs[p], 16)
                for gw in range(8):
                    ins = red(q_sum[:, 8 * gw:8 * gw + 8],
                              pixels[p % 3][:, 512 * gw:512 * gw + 512].rearrange("p (r gh s) -> p gh r s", r=GS, gh=8), AX.XY, ALU.add)
                link(ins)
                ts(q_mean[:, p, :], q_sum[:, :], 1.0 / KWIN, None, ALU.mult).then_inc(s["q_ready"], 1)

            def head_queries(p):
                dve.wait_ge(s["qp_ps"], p + 1)
                nc.vector.scalar_tensor_tensor(
                    q_head[:, :, :], bank[6][:, 0:WIN].unsqueeze(2).broadcast_to([128, WIN, 16]), wt("tok_bq"),
                    wt("headsel").unsqueeze(1).broadcast_to([128, WIN, 16]), ALU.add, ALU.mult).then_inc(s["qhead_ready"], 1)

            def key_bias(p):
                dve.wait_ge(s["qk_ps"], p + 1)
                copy(qb_sb[:, :], bank[6][:, 64:80]).then_inc(s["qb_ready"], 1)

            def center(p):
                dve.wait_ge(s["s_ps"], p + 1)
                dve.wait_ge(s["qb_ready"], p + 1)
                if p:
                    dve.wait_ge(s["pT_ps"], p)
                for k in range(2):
                    ins = tt(sc_sb[:, 8 * k:8 * k + 8, :], bank[2 + k][:, :].rearrange("p (g k) -> p g k", k=64),
                             qb_sb[:, 8 * k:8 * k + 8].unsqueeze(2).broadcast_to([128, 8, 64]), ALU.add)
                link(ins)
                link(red(mx_sb[:, :], sc_sb[:, :, :], AX.X, ALU.max))
                tt(sc_sb[:, :, :], sc_sb[:, :, :], mx_sb[:, :].unsqueeze(2).broadcast_to([128, 16, 64]), ALU.subtract)\
                    .then_inc(s["centered"], 1)

            def normalise(p):
                dve.wait_ge(s["exped"], p + 1)
                link(red(sm_sb[:, :], sc_sb[:, :, :], AX.X, ALU.add))
                link(nc.vector.reciprocal(sm_sb[:, :], sm_sb[:, :]))
                tt(sc_sb[:, :, :], sc_sb[:, :, :], sm_sb[:, :].unsqueeze(2).broadcast_to([128, 16, 64]), ALU.mult)\
                    .then_inc(s["probs"], 1)

            def spread_probabilities(p):
                dve.wait_ge(s["pT_ps"], p + 1)
                if p:
                    dve.wait_ge(s["cx_ps"], p)
                else:
                    dve.wait_ge(s["consts_set"], 4)
                for w in range(2):
                    for k in range(2):
                        ins = copy(pT_sb[64 * w:64 * w + 64, 16 * k:16 * k + 16, w, :],
                                   bank[2 + k][64 * w:64 * w + 64, :].rearrange("p (c j) -> p c j", j=32)[:, :, 0:16])
                ins.then_inc(s["pT_ready"], 1)

            def values(p):
                dve.wait_ge(s["v_ps"], p + 1)
                link(tt(vm_sb[:, :, :], bank[7][:, :].rearrange("p (n h) -> p n h", h=8),
                        wt("headsel8").unsqueeze(1).broadcast_to([128, WIN, 8]), ALU.mult))
                link(red(ctx_sb[:, :], vm_sb[:, :, :], AX.X, ALU.add))
                ts(ctx_sb[:, :], ctx_sb[:, :], wt("tok_bv"), None, ALU.add).then_inc(s["ctx_ready"], 1)

            def add_queries(p):
                dve.wait_ge(s["o_ps"], p + 1)
                nc.vector.scalar_tensor_tensor(hT_sb[:, :], bank[7][:, 0:WIN], wt("tok_bo"), q_mean[:, p, :], ALU.add, ALU.add).then_inc(s["hT_ready"], 1)
            means(0)
            head_queries(0)
            key_bias(0)
            means(1)
            center(0)
            normalise(0)
            for p in range(PAIRS):
                if p + 1 < PAIRS:
                    head_queries(p + 1)
                spread_probabilities(p)
                if p + 1 < PAIRS:
                    key_bias(p + 1)
                if p:
                    add_queries(p - 1)
                if p + 1 < PAIRS:
                    center(p + 1)
                    if p + 2 < PAIRS:
                        means(p + 2)
                    normalise(p + 1)
                values(p)
            add_queries(PAIRS - 1)

            def norm(n, src, dst, then):
                link(red(ln_s[:, :], src, AX.X, ALU.add))
                link(ts(ln_m[:, :], ln_s[:, :], 1.0 / D, None, ALU.mult))
                tt(xc[:, :, :], src, ln_m[:, :].unsqueeze(2).broadcast_to([128, L, D]), ALU.subtract)\
                    .then_inc(s["ln_centered"], 1)
                dve.wait_ge(s["ln_squared"], n + 1)
                link(red(ln_q[:, :], sq[:, :, :], AX.X, ALU.add))
                ts(ln_v[:, :], ln_q[:, :], 1.0 / D, EPS, ALU.mult, ALU.add).then_inc(s["ln_var"], 1)
                dve.wait_ge(s["ln_rstd"], n + 1)
                dve.wait_ge(s["ln_centered"], n + 1)
                tt(dst, xc[:, :, :], rstd[:, :].unsqueeze(2).broadcast_to([128, L, D]), ALU.mult).then_inc(s[then], 1)

            def u_blocks(r):
                dve.wait_ge(s["uT_ps"], r + 1)
                copy(uT[:, 512:768], bank[1][:, 0:256]).then_inc(s["uTb_ready"], 1)
            dve.wait_ge(s["res_in"], 16)
            norm(0, hL[:, :, :], y1[:, :, :], "u_ready")
            u_blocks(0)
            dve.wait_ge(s["lin_ps"], 1)
            for k in range(2):
                ins = tt(half_bank(hs, k), bank_tokens(k, 2), ws("bin").unsqueeze(1).broadcast_to([128, rows(k), D]), ALU.add)
            ins.then_inc(s["u_ready"], 1)
            u_blocks(1)
            for l in range(SSM_LAYERS):
                state = bank[5][0:64, 0:128].rearrange("p (b k) -> p b k", k=CK)
                for k, dst in enumerate((X0, X1)):
                    dve.wait_ge(s["f_ps"], 3 * l + k + 1)
                    copy(dst[:, :, :], state).then_inc(s["x_copied"], 1)
                dve.wait_ge(s["f_ps"], 3 * l + 3)
                for k in range(4):
                    by = 1 + 4 * k
                    ins = copy(XS[:, k, :, by:CK], state[:, :, 0:CK - by])
                ins.then_inc(s["xs_ready"], 1)
                dve.wait_ge(s["c_ps"], l + 1)
                link(copy(c_sb[:, :], bank[4][:, 0:L]))
                for k in range(2):
                    ins = tt(half_bank(y1, k), bank_tokens(k, 2),
                             (c_sb[:, 0:8] if k == 0 else c_sb[:, 8:L]).unsqueeze(2).broadcast_to([128, rows(k), D]), ALU.add)
                ins.then_inc(s["y_ready"], 1)
                dve.wait_ge(s["gelu_ready"], l + 1)
                link(tt(y1[:, :, :], sq[:, :, :], hs[:, :, :], ALU.add))
                norm(l + 1, y1[:, :, :], hs[:, :, :], "u_ready")
                if l + 1 < SSM_LAYERS:
                    u_blocks(l + 2)
            dve.wait_ge(s["u_ready"], 2 + SSM_LAYERS)
            norm(5, hs[:, :, :], y1[:, :, :], "u_ready")
            u_blocks(5)
            dve.wait_ge(s["wout_ps"], 1)
            dve.wait_ge(s["hLb_ready"], 1)
            for k in range(2):
                ins = tt(half_bank(hL, k), bank_tokens(k, 2), half_bank(hL, k), ALU.add)
            ins.then_inc(s["h_ready"], 1)

            dve.wait_ge(s["h_ready"], 1)
            norm(6, hL[:, :, :], x2[:, :, :], "x2_ready")
            u_blocks(6)
            dve.wait_ge(s["x2_ready"], 1)
            dve.wait_ge(s["ffn_in"], 32)
            link(tt(xc[:, :, :], x2[:, :, :], wf("wr").unsqueeze(1).broadcast_to([128, L, D]), ALU.mult))
            link(red(tok_w[:, :], xc[:, :, :], AX.X, ALU.add))
            link(ts(tok_w[:, :], tok_w[:, :], wf("br"), None, ALU.add))
            tt(w_all4[:, :, :], tok_w[:, :].unsqueeze(1).broadcast_to([128, CK, L]),
               wf("isck").unsqueeze(2).broadcast_to([128, CK, L]), ALU.mult).then_inc(s["wexp_ready"], 1)
            dve.wait_ge(s["wall_ps"], 1)
            copy(w_all[:, :], bank[1][:, 256:256 + T + L]).then_inc(s["wall_ready"], 1)
            dve.wait_ge(s["wall_ready"], 1)
            every = w_all[:, 0:T].unsqueeze(1).broadcast_to([128, L, T])
            own = w_all[:, T:T + L].unsqueeze(2).broadcast_to([128, L, T])
            tt(ahead[:, :, :], every, own, ALU.is_gt)
            link(tt(tied[:, :, :], every, own, ALU.is_ge))
            dve.wait_ge(s["ffn_in"], 32)
            link(tt(tied[:, :, :], tied[:, :, :], earlier[:, :, :], ALU.mult))
            link(tt(ahead[:, :, :], ahead[:, :, :], tied[:, :, :], ALU.max))
            link(red(rank[:, :], ahead[:, :, :], AX.X, ALU.add))
            link(nc.vector.scalar_tensor_tensor(w_sel[:, :], rank[:, :], float(CAP), tok_w[:, :], ALU.is_lt, ALU.mult))
            dve.wait_ge(s["ff2_ps"], 1)
            for k in range(2):
                ins = tt(half_bank(y1, k), bank_tokens(k, 0), wf("b2").unsqueeze(1).broadcast_to([128, rows(k), D]), ALU.add)
            link(ins)
            link(tt(y1[:, :, :], y1[:, :, :], w_sel[:, :].unsqueeze(2).broadcast_to([128, L, D]), ALU.mult))
            dve.wait_ge(s["hx_ready"], 1)
            tt(hL[:, :, :], y1[:, :, :], hs[:, :, :], ALU.add).then_inc(s["h2_ready"], 1)

            dve.wait_ge(s["h2_ready"], 1)
            norm(7, hL[:, :, :], x3[:, :, :], "x3_ready")
            dve.wait_ge(s["xN_ps"], 1)
            copy(tokens_of(2), bank[2][0:64, :].rearrange("p (i t) -> p t i", i=4)).then_inc(s["xN_ready"], 1)

            def value(b):
                dve.wait_ge(s["QKV_ps"], 3 * b + 3)
                copy(V[:, b % 2, :, :, 0:AD], bank[0][0:HALF, :].rearrange("p (a h d) -> p a h d", a=2, h=AH))\
                    .then_inc(s["V_ready"], 1)

            def key(b):
                dve.wait_ge(s["QKV_ps"], 3 * b + 2)
                for k in (0, 1):
                    q = slice(AD * k, AD * k + AD)
                    ins = copy(KT[q, b % 2, :, k, :], bank[0][q, 0:2 * T].rearrange("p (m t) -> p m t", m=2))
                ins.then_inc(s["K_ready"], 1)
            dve.wait_ge(s["ones_set"], 2)
            key(0)
            value(0)
            for n in range(UNITS + 5):
                b, slot = divmod(n, 6)
                if b and slot == 2:
                    dve.wait_ge(s["PV_ps"], 6 * b)
                    if b >= 2:
                        dve.wait_ge(s["oT_ps"], b - 1)
                    for a in range(2):
                        o = bank[1 + a][0:HALF, 0:AH * (AD + 1)].rearrange("p (h d) -> p h d", h=AH)
                        link(nc.vector.reciprocal(o_inv[:, a, :], o[:, :, AD]))
                        ins = tt(o_n[:, a, :, :], o[:, :, 0:AD], o_inv[:, a, :].unsqueeze(2).broadcast_to([HALF, AH, AD]), ALU.mult)
                    ins.then_inc(s["o_ready"], 1)
                if n < UNITS:
                    heads, keys = unit_shape(n)
                    dve.wait_ge(s["S_ps"], n + 1)
                    scores = bank[5 + n % 3][0:HALF, 0:UNIT].rearrange("p (h k) -> p h k", h=heads)
                    link(red(S_max[:, n % 3, 0:heads], scores, AX.X, ALU.max))
                    if n >= 3:
                        dve.wait_ge(s["PT_ps"], n - 2)
                    tt(S[:, n % 3, :].rearrange("p (h k) -> p h k", h=heads), scores,
                       S_max[:, n % 3, 0:heads].unsqueeze(2).broadcast_to([HALF, heads, keys]), ALU.subtract)\
                        .then_inc(s["S_centered"], 1)
                if b + 1 < B and slot == 1:
                    key(b + 1)
                if b + 1 < B and slot == 2:
                    value(b + 1)
                if b and slot == 4:
                    dve.wait_ge(s["wo_ps"], b)
                    dve.wait_ge(s["hb_ready"], 1)
                    h = hN[:, 2 * b - 2:2 * b, :]
                    tt(h, bank[0][0:HALF, 0:2 * D].rearrange("p (a h) -> p a h", a=2), h, ALU.add).then_inc(s["h3_ready"], 1)

            dve.wait_ge(s["res_in"], 48)
            norm(8, hL[:, :, :], x4[:, :, :], "x4_ready")
            dve.wait_ge(s["x4T_ps"], 1)
            copy(x4T[:, 1024:1536], bank[2][0:64, :]).then_inc(s["x4T_ready"], 1)
            dve.wait_ge(s["late_in"], LATE)
            dve.wait_ge(s["logits_ps"], 1)
            for k in range(2):
                ins = tt(half_bank(logits, k), bank_tokens(k, 3), we("rbr").unsqueeze(1).broadcast_to([128, rows(k), D]), ALU.add)
            link(ins)
            for i in range(L):
                ins = nc.vector.max(top[:, i, :], logits[:, i, :])
            link(ins)
            for i in range(L):
                ins = nc.vector.max_index(top_e[:, i, :], top[:, i, :], logits[:, i, :])
            link(ins)
            tt(gate[:, 0, :], top[:, :, 1], top[:, :, 0], ALU.subtract).then_inc(s["top_gap"], 1)
            link(copy(top_b[:, :, :], top_e[:, :, 0:2]))
            for k in range(2):
                ins = tt(OH[:, k, :, :], wb("iota_e").unsqueeze(1).broadcast_to([128, L, E]),
                         top_b[:, :, k].unsqueeze(2).broadcast_to([128, L, E]), ALU.is_equal)
            link(ins)
            tt(OH[:, 2, :, :], OH[:, 0, :, :], OH[:, 1, :, :], ALU.add).then_inc(s["oh_ready"], 1)
            dve.wait_ge(s["gap_exped"], 1)
            link(ts(gate[:, 0, :], gate[:, 1, :], 1.0, None, ALU.add))
            link(nc.vector.reciprocal(gate[:, 2, :], gate[:, 0, :]))
            tt(gate[:, 3, :], gate[:, 2, :], gate[:, 1, :], ALU.mult)
            dve.wait_ge(s["rank_ps"], 1)
            link(tt(blk_cmp[:, 0:TOK // BLK], bank[7][0:64, 0:1].broadcast_to([64, TOK // BLK]), wm("steps")[0:64, :], ALU.is_gt))
            link(red(n_blk[:, :], blk_cmp[:, 0:TOK // BLK], AX.X, ALU.add))
            ts(n_bc[:, :], wm("ones")[0:64, :], n_blk[:, 0:1], None, ALU.mult).then_inc(s["nblk_ready"], 1)
            dve.wait_ge(s["base_ps"], 1)
            link(copy(base[:, :], bank[7][:, 64:128]))
            link(copy(end[:, :], bank[7][0:64, 1:2]))
            ts(blk_cmp[:, :], wm("iota_m")[0:64, :], end[:, 0:1], None, ALU.is_ge).then_inc(s["nblk_ready"], 1)
            for k in range(2):
                ins = tt(half_bank(xc, k), bank_tokens(k, 5), base[:, :].unsqueeze(1).broadcast_to([128, rows(k), D]), ALU.add)
            link(ins)
            for k in range(2):
                link(tt(sq[:, :, :], xc[:, :, :], OH[:, k, :, :], ALU.mult))
                link(red(slot_f[:, k, :], sq[:, :, :], AX.X, ALU.add))
            link(copy(slot_i[:, 0, :, :], slot_f[:, :, :]))
            ts(slot_i[:, 1, :, :], slot_i[:, 0, :, :], 127, None, ALU.bitwise_and)
            link(ts(slot_i[:, 2, :, :], slot_i[:, 0, :, :], 7, None, ALU.logical_shift_right))
            nc.vector.scalar_tensor_tensor(addr[:, :, :], slot_i[:, 1, :, :], float(SLOTS // 128), slot_i[:, 2, :, :],
                                           ALU.mult, ALU.add).then_inc(s["addr_ready"], 1)
            dve.wait_ge(s["blke_ps"], 1)
            ts(blk_e[:, :], bank[7][0:1, 128:128 + NBLK], float(E - 1), None, ALU.min).then_inc(s["blke_ready"], 1)
            dve.wait_ge(s["addr_ready"], 1)
            link(tt(xc[:, :, :], OH[:, 0, :, :], gate[:, 2, :].unsqueeze(2).broadcast_to([128, L, E]), ALU.mult))
            link(tt(sq[:, :, :], OH[:, 1, :, :], gate[:, 3, :].unsqueeze(2).broadcast_to([128, L, E]), ALU.mult))
            tt(y1[:, :, :], xc[:, :, :], sq[:, :, :], ALU.add).then_inc(s["cmb_ready"], 1)
            dve.wait_ge(s["cmbT_ps"], 1)
            copy(x4T[:, 1024:1536], bank[2][0:64, :]).then_inc(s["cmbT_ready"], 1)
            dve.wait_ge(s["b2_ps"], 1)
            for k in range(2):
                ins = tt(half_bank(hL, k), bank_tokens(k, 3), half_bank(hL, k), ALU.add)
            ins.then_inc(s["b2_added"], 1)
            dve.wait_ge(s["wall_in"], 16)
            dve.wait_ge(s["blke_ready"], 1)
            dve.sem_inc(s["y8_ready"], 2)
            for k in range(2):
                dve.sem_inc(y8_out[k], 16)
            regs = [dve.alloc_register(f"expert{k}") for k in range(GB)]
            with dve.Fori(0, GROUPS // 2) as pair:
                for u in range(2):
                    g = pair * 2 + u
                    dve.load(regs, blk_e[0:1, bass.ds(g * GB, GB)])
                    for k in range(GB):
                        e = dve.snap(regs[k], min_val=0, max_val=E - 1)
                        ins = copy(W_sb[:, u, k, :], big[:, bass.ds(e * EW, EW)])
                    ins.then_inc(s["W8_ready"], 1)
                    dve.wait_ge(s["y8_ps"], g + 1)
                    dve.wait_ge(y8_out[u], pair * 16 + 16)
                    copy(y_g[:, u, :, :], bank[4 + u][:, 0:256].rearrange("p (q h) -> p q h", h=D)).then_inc(s["y8_ready"], 1)
            dve.wait_ge(s["b2_added"], 1)
            for i in range(L):
                if i % 2 == 0:
                    dve.wait_ge(gathered[i // 2], 16 * 4)
                link(nc.vector.scalar_tensor_tensor(hL[:, i, :], y_back[:, 0, i, :], gate[:, 2, i:i + 1], hL[:, i, :], ALU.mult, ALU.add))
                ins = nc.vector.scalar_tensor_tensor(hL[:, i, :], y_back[:, 1, i, :], gate[:, 3, i:i + 1], hL[:, i, :], ALU.mult, ALU.add)
                if i % 6 == 5:
                    ins.then_inc(s["out_ready"], 1)

        @block.tensor
        def _(pe):
            def mm(out, lhsT, rhs, start=True, stop=True, **kw):
                return nc.tensor.matmul(out, lhsT, rhs, start=start, stop=stop, **kw)

            def transpose(out, in_, n):
                return nc.tensor.transpose(out, in_, ident[0:n, 0:n])

            pe.wait_ge(s["zero_set"], 1)
            for k in range(WARM_UP):
                mm(bank[6][0:64, :], zero[:, :], zero[:, :].unsqueeze(1).broadcast_to([128, 8, 64]))

            pe.wait_ge(s["first_in"], 32)
            for l in range(SSM_LAYERS):
                ins = mm(bank[7][0:64, l:l + 1], wa("C", l), wt("mean")[0:64, :])
            ins.then_inc(s["cbar_ps"], 1)

            def level(n):
                m, a, b = LEVELS[n]
                if n:
                    pe.wait_ge(s["pow_ready"], n)
                for l in range(SSM_LAYERS):
                    mm(bank[0][0:64, 128 * l:128 * l + 64], tra(a, l), nat(b, l))
                    ins = mm(bank[0][0:64, 128 * l + 64:128 * l + 128], nat(b, l), tra(a, l))
                ins.then_inc(s["pow_ps"], 1)

            def extend(n):
                m = 1 << n
                k = min(m, L - m)
                pe.wait_ge(s["z_ready"], n + 1)
                for l in range(SSM_LAYERS):
                    ins = mm(bank[1 + l][0:64, 0:65 * k], nat(m, l), Z[:, l, 0:k, :])
                ins.then_inc(s["z_ps"], 1)
            for n in range(4):
                level(n)
                extend(n)
            level(4)
            level(5)

            def scan_matrices(l):
                pe.wait_ge(s["xT_ready"], 8 * (l + 1))
                mm(bank[0][:, :], wa("BB", l), Z[:, l, 0:8, 0:64])
                mm(bank[1][:, 0:256], wa("BB", l), Z[:, l, 8:12, 0:64])
                ins = mm(bank[1][:, 256:256 + L - 1], wa("BB", l), Z[:, l, 0:L - 1, 64])
                if l:
                    pe.wait_ge(s["r_ready"], l)
                    for m in range(SSM_LAYERS):
                        ins = mm(bank[1][0:64, 320 + L * m:320 + L * m + L], nat(48, m), R[:, m, l - 1, :])
                ins.then_inc(s["mt_ps"], 1)

            def chunk(p, c):
                return xw[p % 2][:, 2 * c:2 * c + 2, :].rearrange("p n k -> p (n k)")

            def x_blocks(p, blocks):
                for g in blocks:
                    if g < POOL_ROWS:
                        pe.wait_ge(s["xw_pool_ready"], POOL_ROWS * p + g + 1)
                    else:
                        pe.wait_ge(s["xw_act_ready"], (8 - POOL_ROWS) * p + g - POOL_ROWS + 1)
                    n = 8 * p + g
                    if n >= 2:
                        pe.wait_ge(s["xT_ready"], n - 1)
                    if p and g == 0:
                        pe.wait_ge(s["r_ready"], p)
                        pe.wait_ge(s["mt_ready"], 1)
                    for k in range(4):
                        ins = transpose(bank[g % 2][:, 128 * k:128 * k + 128], chunk(p, 4 * g + k), 128)
                    ins.then_inc(s["xT_ps"], 1)

            def project_queries(p):
                pe.wait_ge(s["q_ready"], p + 1)
                if p:
                    pe.wait_ge(s["qb_ready"], p)
                mm(bank[6][:, 0:WIN], wt("tok_WqT"), q_mean[:, p, :]).then_inc(s["qp_ps"], 1)

            def slots():
                return [(2 * (4 * t + j) + w, j, 2 * t + w) for t in range(8) for w in range(2) for j in range(4)]

            def keyed_queries(p):
                pe.wait_ge(s["qhead_ready"], p + 1)
                if p >= 2:
                    pe.wait_ge(s["cx_ready"], p - 1)
                mm(bank[4][:, :], wt("tok_Wk"), head_buf[:, 0:512])
                mm(bank[5][:, :], wt("tok_Wk"), head_buf[:, 512:1024])
                pe.wait_ge(s["pads_set"], 2)
                for n, j, slot in slots():
                    ins = mm(bank[6][32 * j:32 * j + 32, 64 + slot:65 + slot], head_buf[:, 16 * n:16 * n + 32], wt("tok_bk"))
                ins.then_inc(s["qk_ps"], 1)

            def scores(p):
                pe.wait_ge(s["xw_pool_ready"], POOL_ROWS * (p + 1))
                pe.wait_ge(s["xw_act_ready"], (8 - POOL_ROWS) * (p + 1))
                pe.wait_ge(s["qk_ready"], p + 1)
                if p:
                    pe.wait_ge(s["pT_ready"], p)
                for n, j, slot in slots():
                    ins = mm(bank[2 + slot // 8][32 * j:32 * j + 32, 64 * (slot % 8):64 * (slot % 8) + 64],
                             qk_sb[:, 16 * n:16 * n + 32], xw[p % 2][:, n, :])
                ins.then_inc(s["s_ps"], 1)

            def turn_probabilities(p):
                pe.wait_ge(s["probs"], p + 1)
                for t in range(8):
                    ins = transpose(bank[2 + t // 4][:, 128 * (t % 4):128 * (t % 4) + 128],
                                    sc_sb[:, 2 * t:2 * t + 2, :].rearrange("p w k -> p (w k)"), 128)
                ins.then_inc(s["pT_ps"], 1)

            def weighted_pixels(p):
                pe.wait_ge(s["pT_ready"], p + 1)
                pe.wait_ge(s["xT_ready"], 8 * (p + 1))
                for c in range(CHUNKS):
                    t, j = divmod(c, 4)
                    ins = mm(bank[4 + t // 4][32 * j:32 * j + 32, 128 * (t % 4):128 * (t % 4) + 128],
                             pT_sb[:, c, :, :].rearrange("p w j -> p (w j)"), xT[p % 2][:, 128 * c:128 * c + 128])
                ins.then_inc(s["cx_ps"], 1)

            def turn_weighted(p):
                pe.wait_ge(s["raw_ready"], p + 1)
                for t in range(8):
                    ins = transpose(bank[4 + t // 4][:, 128 * (t % 4):128 * (t % 4) + 128], raw_sb[:, 128 * t:128 * t + 128], 128)
                ins.then_inc(s["turned_ps"], 1)

            def project_values(p):
                pe.wait_ge(s["cx_ready"], p + 1)
                if p:
                    pe.wait_ge(s["hn_ready"], p)
                mm(bank[7][:, :], wt("tok_WvT"), cx_sb[:, :, :].rearrange("p n h -> p (n h)")).then_inc(s["v_ps"], 1)

            def project_out(p):
                pe.wait_ge(s["ctx_ready"], p + 1)
                mm(bank[7][:, 0:WIN], wt("tok_WoT"), ctx_sb[:, :]).then_inc(s["o_ps"], 1)

            def turn_tokens(p):
                pe.wait_ge(s["hT_ready"], p + 1)
                transpose(bank[7][0:64, 64:192], hT_sb[:, :], 128).then_inc(s["hn_ps"], 1)

            pe.wait_ge(s["pow_ready"], 6)
            pe.wait_ge(s["z_ready"], 5)
            project_queries(0)
            keyed_queries(0)
            x_blocks(0, range(8))
            scores(0)
            scan_matrices(0)
            for p in range(PAIRS):
                if p + 1 < PAIRS:
                    project_queries(p + 1)
                turn_probabilities(p)
                if p + 1 < PAIRS:
                    keyed_queries(p + 1)
                    x_blocks(p + 1, range(4))
                if p:
                    project_out(p - 1)
                if p + 1 < PAIRS:
                    scores(p + 1)
                if p:
                    turn_tokens(p - 1)
                weighted_pixels(p)
                if p + 1 < PAIRS:
                    x_blocks(p + 1, range(4, 6))
                turn_weighted(p)
                if p + 1 < PAIRS:
                    x_blocks(p + 1, range(6, 8))
                project_values(p)
                if p + 1 < PAIRS:
                    scan_matrices(p + 1)
            project_out(PAIRS - 1)
            turn_tokens(PAIRS - 1)

            def u_blocks(r, src):
                for j in range(NPAIR):
                    ins = transpose(bank[j // 4][:, 128 * (j % 4):128 * (j % 4) + 128],
                                    src[:, 2 * j:2 * j + 2, :].rearrange("p i h -> p (i h)"), 128)
                ins.then_inc(s["uT_ps"], 1)

            def u(j):
                return uT[:, 128 * j:128 * j + 128]

            def project(w):
                for j in range(NPAIR):
                    ins = mm(bank[2 + j // 4][:, 128 * (j % 4):128 * (j % 4) + 128], u(j), w)
                return ins
            pe.wait_ge(s["u_ready"], 1)
            u_blocks(0, y1)
            pe.wait_ge(s["uTa_ready"], 1)
            pe.wait_ge(s["uTb_ready"], 1)
            pe.wait_ge(s["wssm_in"], 16)
            project(ws("WinT")).then_inc(s["lin_ps"], 1)
            pe.wait_ge(s["u_ready"], 2)
            u_blocks(1, hs)
            pe.wait_ge(s["r_ready"], SSM_LAYERS)
            for l in range(SSM_LAYERS):
                pe.wait_ge(s["uTa_ready"], l + 2)
                pe.wait_ge(s["uTb_ready"], l + 2)
                state = bank[5][0:64, 0:128].rearrange("p (b k) -> p b k", k=CK)
                for j in range(NPAIR):
                    ins = mm(bank[5][0:64, 0:128], WS[:, l, NPAIR - 1 - j, :], u(j), start=j == 0, stop=j == NPAIR - 1)
                ins.then_inc(s["f_ps"], 1)
                project(ws(f"DT{l}"))
                for j in range(NPAIR):
                    ins = mm(bank[4][:, 0:L], u(j), KZ[:, l, L - 1 - 2 * j:2 * L - 1 - 2 * j], start=j == 0, stop=False,
                             skip_group_check=True)
                for k, (m, X, by) in enumerate(((12, X0, 1), (24, X1, 2))):
                    pe.wait_ge(s["x_copied"], 2 * l + k + 1)
                    mm(state[:, :, by:CK], tra(m, l), X[:, :, 0:CK - by], start=False, stop=True, skip_group_check=True)\
                        .then_inc(s["f_ps"], 1)
                pe.wait_ge(s["xs_ready"], l + 1)
                for k in range(4):
                    ins = mm(bank[4][:, 0:L], XS[:, k, :, :].rearrange("p b k -> p (b k)"), R[:, l, k, :], start=False, stop=k == 3,
                             skip_group_check=True)
                ins.then_inc(s["c_ps"], 1)
                if l + 1 < SSM_LAYERS:
                    pe.wait_ge(s["u_ready"], l + 3)
                    u_blocks(l + 2, hs)
            pe.wait_ge(s["u_ready"], 3 + SSM_LAYERS)
            u_blocks(5, y1)
            pe.wait_ge(s["uTa_ready"], 6)
            pe.wait_ge(s["uTb_ready"], 6)
            project(ws("WoutT")).then_inc(s["wout_ps"], 1)

            pe.wait_ge(s["x2_ready"], 1)
            u_blocks(6, x2)
            pe.wait_ge(s["uTa_ready"], 7)
            pe.wait_ge(s["uTb_ready"], 7)
            pe.wait_ge(s["ffn_in"], 32)
            pe.wait_ge(s["h_ready"], 1)
            for g in range(4):
                par, mt = g // 2, g % 2
                q = slice(64 * par, 64 * par + 64)
                for k in range(2):
                    n = 512 if k == 0 else 256
                    if 2 * g + k >= 6:
                        pe.wait_ge(s["ff1_ready"], 2 * g + k - 5)
                    mm(bank[2 + (2 * g + k) % 6][:, 0:n], wf("w1")[q, 128 * mt:128 * mt + 128],
                       uT[q, 512 * k:512 * k + n]).then_inc(s["ff1_ps"], 1)
            pe.wait_ge(s["wexp_ready"], 1)
            mm(bank[1][:, 256:256 + T], wf("sameb"), w_all4[:, :, :].rearrange("p k i -> p (k i)"))
            mm(bank[1][:, 256 + T:256 + T + L], ident, tok_w[:, :]).then_inc(s["wall_ps"], 1)
            pe.wait_ge(s["ff1_ready"], 8)
            pe.wait_ge(s["wall_ready"], 1)
            for i in range(L):
                for mt in range(2):
                    ins = mm(bank[i // 8][:, 64 * (i % 8):64 * (i % 8) + 64],
                             G[:, mt, i % 2, 128 * (i // 2):128 * (i // 2) + 128],
                             wf("w2")[:, 64 * mt:64 * mt + 64], start=mt == 0, stop=mt == 1)
            ins.then_inc(s["ff2_ps"], 1)

            pe.wait_ge(s["x3_ready"], 1)
            pe.wait_ge(s["h2_ready"], 1)
            for i in range(L):
                ins = transpose(bank[i // 4][0:64, 128 * (i % 4):128 * (i % 4) + 128], x3[:, i, :], 128)
            ins.then_inc(s["xN_ps"], 1)
            pe.wait_ge(s["xN_ready"], 2)
            pe.wait_ge(s["late_in"], LATE)

            def tokens(b):
                return xN[:, b, :, :].rearrange("p k i -> p (k i)")

            def qk(b, which):
                if which:
                    pe.wait_ge(s["Q_ready"], b + 1)
                for m in range(2):
                    ins = mm(bank[0][:, T * m:T * m + T], w_att[:, which, m, :], tokens(b))
                ins.then_inc(s["QKV_ps"], 1)

            def value(b):
                pe.wait_ge(s["K_ready"], 2 * b + 2)
                for a in range(2):
                    ins = mm(bank[0][0:HALF, 2 * 128 * a:2 * 128 * a + 256], tokens(b)[:, HALF * a:HALF * a + HALF],
                             w_att[:, 2, :, :].rearrange("p m n -> p (m n)"))
                ins.then_inc(s["QKV_ps"], 1)
            qk(0, 0)
            qk(0, 1)
            value(0)
            pe.wait_ge(s["V_ready"], 1)
            pe.wait_ge(s["ones_set"], 2)
            for n in range(UNITS + 5):
                b, slot = divmod(n, 6)
                if n < UNITS:
                    heads, keys = unit_shape(n)
                    h0, a = unit_of(n)
                    if n >= 3:
                        pe.wait_ge(s["S_centered"], n - 2)
                    dst = bank[5 + n % 3][0:HALF, 0:UNIT]
                    mm(dst, identb[:, :], alibi[:, h0:h0 + heads, T - keys:T], start=True, stop=False, skip_group_check=True)
                    mm(dst, QT[:, b % 2, h0 // 4, HALF * a:HALF * a + HALF],
                       KT[:, b % 2, h0 // 4, h0 % 4:h0 % 4 + heads, 0:keys], start=False, stop=True,
                       skip_group_check=True).then_inc(s["S_ps"], 1)
                if b + 1 < B and slot in (0, 1):
                    if slot == 0 and b >= 2:
                        pe.wait_ge(s["h3_ready"], b - 1)
                    qk(b + 1, slot)
                if b + 1 < B and slot == 2:
                    value(b + 1)
                if b and slot == 3:
                    pe.wait_ge(s["o_ready"], b)
                    pe.wait_ge(s["V_ready"], min(b + 2, B))
                    for k in range(4):
                        ins = transpose(bank[0][:, HALF * k:HALF * k + HALF],
                                        o_n[:, k // 2, 4 * (k % 2):4 * (k % 2) + 4, :].rearrange("p h d -> p (h d)"), HALF)
                    ins.then_inc(s["oT_ps"], 1)
                if b and slot == 4:
                    pe.wait_ge(s["oT_ready"], b)
                    for a in range(2):
                        for k in range(2):
                            ins = mm(bank[0][0:HALF, D * a:D * a + D], oT[:, 2 * a + k, :], we("Wo")[:, D * k:D * k + D],
                                     start=k == 0, stop=k == 1)
                    ins.then_inc(s["wo_ps"], 1)
                if 1 <= n <= UNITS:
                    m = n - 1
                    pe.wait_ge(s["S_exped"], m + 1)
                    if m >= 2:
                        pe.wait_ge(s["PT_ready"], m - 1)
                    for k in range(4):
                        ins = transpose(bank[3 + m % 2][0:HALF, HALF * k:HALF * k + HALF],
                                        S[:, m % 3, HALF * k:HALF * k + HALF], HALF)
                    ins.then_inc(s["PT_ps"], 1)
                if 2 <= n < UNITS + 2:
                    m = n - 2
                    heads, keys = unit_shape(m)
                    h0, a = unit_of(m)
                    pe.wait_ge(s["PT_ready"], m + 1)
                    if m % 6 == 0 and m:
                        pe.wait_ge(s["o_ready"], m // 6)
                    parts = keys // HALF
                    for k in range(heads):
                        for c in range(parts):
                            at = HALF * (parts * k + c)
                            ins = mm(bank[1 + a][0:HALF, (AD + 1) * (h0 + k):(AD + 1) * (h0 + k + 1)],
                                     PT[:, m % 2, at:at + HALF], V[:, (m // 6) % 2, c, h0 + k, :],
                                     start=c == 0, stop=c == parts - 1)
                    ins.then_inc(s["PV_ps"], 1)

            pe.wait_ge(s["x4_ready"], 1)

            def blocks64(src, then):
                for i in range(L):
                    ins = transpose(bank[i // 4][0:64, 128 * (i % 4):128 * (i % 4) + 128], src[:, i, :], 128)
                ins.then_inc(s[then], 1)
            blocks64(x4, "x4T_ps")
            pe.wait_ge(s["x4T_ready"], 2)
            pe.wait_ge(s["late_in"], LATE)
            for i in range(L):
                ins = mm(bank[3 + i // 8][:, 64 * (i % 8):64 * (i % 8) + 64], x4T[:, 128 * i:128 * i + 128], we("Wr")[0:64, :])
            ins.then_inc(s["logits_ps"], 1)
            pe.wait_ge(s["oh_ready"], 1)
            for k in range(2):
                lo, hi = (0, 8) if k == 0 else (8, L)
                dst = bank[5 + k]
                mm(dst[:, 0:64 * (hi - lo)], wb("before"), OH[:, 2, lo:hi, :], start=True, stop=False, skip_group_check=True)
                for i in range(hi - 1):
                    a = max(lo, i + 1)
                    mm(dst[:, 64 * (a - lo):64 * (hi - lo)], wb("ones_b"),
                       OH[:, 2, i, :].unsqueeze(1).broadcast_to([128, hi - a, E]),
                       start=False, stop=i == hi - 2, skip_group_check=True)
            for i in range(L):
                ins = mm(bank[7][0:64, 0:1], OH[:, 2, i, :], wb("ones_b")[:, 0:1], start=i == 0, stop=i == L - 1)
            ins.then_inc(s["rank_ps"], 1)
            pe.wait_ge(s["nblk_ready"], 1)
            mm(bank[7][:, 64:128], n_bc[:, :], wm("before_e")[0:64, :])
            mm(bank[7][0:64, 1:2], wm("upto_e")[0:64, :], n_blk[:, :]).then_inc(s["base_ps"], 1)
            pe.wait_ge(s["nblk_ready"], 2)
            mm(bank[7][0:1, 128:128 + NBLK], wm("ones")[0:64, 0:1], blk_cmp[:, :]).then_inc(s["blke_ps"], 1)
            pe.wait_ge(s["cmb_ready"], 1)
            blocks64(y1, "cmbT_ps")
            pe.wait_ge(s["cmbT_ready"], 2)
            for i in range(L):
                ins = mm(bank[3 + i // 8][:, 64 * (i % 8):64 * (i % 8) + 64], x4T[:, 128 * i:128 * i + 128], wm("b2")[0:64, :])
            ins.then_inc(s["b2_ps"], 1)
            pe.wait_ge(s["b2_added"], 1)
            pe.wait_ge(s["moe_consts"], 1)
            with pe.Fori(0, GROUPS // 2) as pair:
                for u in range(2):
                    g = pair * 2 + u
                    pe.wait_ge(xg_in[u], pair * 16 + 16)
                    pe.sem_inc(s["xg_seen"], 1)
                    for q in range(GB // 2):
                        ins = transpose(bank[u][0:64, 128 * q:128 * q + 128], x_g[:, u, q, :], 128)
                    ins.then_inc(s["xT8_ps"], 1)
                    pe.wait_ge(s["xT8_ready"], g + 3)
                    pe.wait_ge(s["W8_ready"], g + 1)
                    for k in range(GB):
                        ins = mm(bank[2 + u][:, BLK * k:BLK * k + BLK], W_sb[0:D + 1, u, k, 0:EH],
                                 xT_sb[0:D + 1, u, BLK * k:BLK * k + BLK])
                    ins.then_inc(s["h8_ps"], 1)
                    pe.wait_ge(s["h8_ready"], g + 1)
                    pe.wait_ge(s["y8_ready"], g + 1)
                    for k in range(GB):
                        ins = mm(bank[4 + u][64 * (k % 2):64 * (k % 2) + 64, D * (k // 2):D * (k // 2) + D],
                                 h_sb[:, u, BLK * k:BLK * k + BLK], W_sb[:, u, k, EH:EW])
                    ins.then_inc(s["y8_ps"], 1)






def _pack(cols, parts, values):
    out = np.zeros((parts, sum(n for _, n in cols)), np.float32)
    at = 0
    for name, n in cols:
        v = values[name]
        out[:v.shape[0], at:at + n] = v
        at += n
    return out


def _diag2(m):
    out = np.zeros((128, 128), np.float32)
    out[:64, :64] = m
    out[64:, 64:] = m
    return out


def _twice(v):
    return np.concatenate([v, v], axis=0)


def _row(v, parts=128):
    return np.broadcast_to(np.reshape(v, (1, -1)), (parts, v.size))


def _layout(a):
    head = np.zeros((128, 2, NH), np.float32)
    for p in range(128):
        head[p, p // 64, (p % 64) // (D // NH)] = 1.0
    part = np.arange(128)
    f = {
        "w_tok": _pack(WTOK, 128, {
            "ident": np.eye(128, dtype=np.float32), "tok_WqT": _diag2(a["L0_tok_Wq"].T), "tok_Wk": _diag2(a["L0_tok_Wk"]),
            "tok_WvT": _diag2(a["L0_tok_Wv"].T), "tok_WoT": _diag2(a["L0_tok_Wo"].T),
            "tok_bq": _twice(a["L0_tok_bq"][:, None]), "tok_bk": _twice(a["L0_tok_bk"][:, None]),
            "tok_bv": _twice(a["L0_tok_bv"][:, None]), "tok_bo": _twice(a["L0_tok_bo"][:, None]),
            "headsel": head.reshape(128, 16), "headsel8": head[:, 0] + head[:, 1],
            "mean": np.full((128, 1), 1.0 / D, np.float32)}),
        "w_a": np.stack([_pack(WA, 64, {
            "A": a["L0_attn_A"][l], "AT": a["L0_attn_A"][l].T,
            "BB": np.concatenate([a["L0_attn_Bm"][l], a["L0_attn_Bm"][l]], axis=1), "C": a["L0_attn_Cm"][l]})
            for l in range(SSM_LAYERS)], axis=1),
        "w_ssm": _pack(WSSM, 128, {
            "WinT": _diag2(a["L0_attn_Win"].T), "bin": _row(a["L0_attn_bin_"]),
            "WoutT": _diag2(a["L0_attn_Wout"].T), "bout": _row(a["L0_attn_bout"]),
            **{f"DT{l}": _diag2(a["L0_attn_Dm"][l].T) for l in range(SSM_LAYERS)}}),
        "w_ffn": _pack(WFFN, 128, {
            "wr": _row(a["L0_ffn_wr"]), "br": _row(a["L0_ffn_br"]), "w1": _twice(a["L0_ffn_w1"]),
            "b1": a["L0_ffn_b1"].reshape(2, 128).T, "w2": a["L0_ffn_w2"].reshape(2, 128, D).transpose(1, 0, 2).reshape(128, 2 * D),
            "b2": _row(a["L0_ffn_b2"]),
            "sameb": (part[:, None] // CK == part[None, :] // CK).astype(np.float32),
            "isck": (part[:, None] % CK == np.arange(CK)[None, :]).astype(np.float32)}),
    }
    tok = (part % CK)[:, None] * L + np.arange(L)[None, :]
    f["earlier"] = (np.arange(T)[None, None, :] < tok[:, :, None]).astype(mybir.dt.np(BF16))
    f["w_att"] = np.concatenate([a["L1_attn_Wq"], a["L1_attn_Wk"], a["L1_attn_Wv"]], axis=1)
    f["w_exp"] = _pack(WEXP, 128, {
        "Wo": a["L1_attn_Wo"].reshape(2, 128, D).transpose(1, 0, 2).reshape(128, 2 * D), "bo": _row(a["L1_attn_bo"]),
        "Wr": a["L1_ffn_Wr"], "rbr": _row(a["L1_ffn_br"])})
    t, k = np.arange(HALF)[:, None] + HALF, np.arange(T)[None, :]
    slope = 0.5 ** np.arange(1, AH + 1)
    f["alibi"] = np.where((k <= t)[:, None, :], slope[None, :, None] * (k - t)[:, None, :], -1e30).astype(mybir.dt.np(BF16))
    f["identb"] = np.eye(HALF).astype(mybir.dt.np(BF16))
    e = np.arange(E)
    f["w_experts"] = np.zeros((128, E, EW), np.float32)
    f["w_experts"][0:D, :, 0:EH] = a["L1_ffn_W1"].transpose(1, 0, 2)
    f["w_experts"][D, :, 0:EH] = a["L1_ffn_b1"]
    f["w_experts"][:, :, EH:] = a["L1_ffn_W2"].transpose(1, 0, 2)
    f["w_moe"] = _pack(WMOE, 128, {
        "b2": a["L1_ffn_b2"], "before_e": BLK * (e[:, None] < e[None, :]), "upto_e": (e[:, None] <= e[None, :]),
        "iota_m": _row(np.arange(NBLK)), "steps": _row(BLK * np.arange(TOK // BLK)), "ones": np.ones((128, 128))})
    f["w_bit"] = np.concatenate([part[:, None] < part[None, :], np.ones((128, 128)), _row(e)], axis=1).astype(mybir.dt.np(BF16))
    return f


def kernel(**inputs):
    import concourse.bacc as _bacc
    from concourse.bass_utils import run_bass_kernel_spmd as _run

    a = {k: np.asarray(v) for k, v in inputs.items()}
    nc = _bacc.Bacc("TRN2", target_bir_lowering=False, num_devices=1)
    feeds = {"x": a["x"], "txt": a["txt"], **_layout(a)}
    arrays, args = {}, {}
    for name, v in feeds.items():
        v = np.ascontiguousarray(v)
        arrays[f"in_{name}"] = v
        args[name] = nc.dram_tensor(f"in_{name}", v.shape, mybir.dt.from_np(v.dtype), kind="ExternalInput").ap()
    out = nc.dram_tensor("out_0", (B, T, D), F32, kind="ExternalOutput").ap()
    build(nc, args, out)
    r = _run(nc, [arrays], core_ids=[0])
    return r.results[0]["out_0"]
```
